# Optimizing a Trainium2 kernel written in Bass

```python
import numpy as np
import jax
import jax.numpy as jnp

def _softmax(x, axis=-1):
    return jax.nn.softmax(x, axis=axis)

def _gelu(x):
    return jax.nn.gelu(x, approximate=True)

def _silu(x):
    return jax.nn.silu(x)

def _sigmoid(x):
    return jax.nn.sigmoid(x)

def _layernorm(x, axis=-1, eps=1e-05):
    m = jnp.mean(x, axis=axis, keepdims=True)
    v = jnp.var(x, axis=axis, keepdims=True)
    return (x - m) / jnp.sqrt(v + eps)

def _scatter_add(tgt, idx, src, axis=0):
    return tgt.at[idx].add(src)

def _segment_sum(src, seg, n):
    return jax.ops.segment_sum(src, seg, n)
kernel_name = 'mk_adaln_d1_jaxref_r4_c5a041'

def setup_inputs(seed: int=0):
    np.random.seed(seed)
    _w = jnp.asarray

    def _L0_attn_setup():
        import jax, jax.numpy as jnp
        import numpy as np
        D = 256
        E = 2 * D
        N = 64
        R = D // 16
        K = 4
        BATCH, L = (2, 512)
        LN_EPS = 1e-05

        def _layernorm(x, w, b):
            mu = x.mean(-1, keepdims=True)
            var = ((x - mu) ** 2).mean(-1, keepdims=True)
            return (x - mu) * jax.lax.rsqrt(var + LN_EPS) * w + b

        def _silu(x):
            return x * jax.nn.sigmoid(x)

        def _mamba(x, W_in, conv_w, conv_b, W_xp, W_dt, dt_b, A_log, Dp, W_out):
            Bsz = x.shape[0]
            xz = x @ W_in.T
            xp, z = jnp.split(xz, 2, axis=-1)
            xc = jax.lax.conv_general_dilated(xp.transpose(0, 2, 1), conv_w[:, None, :], window_strides=(1,), padding=[(K - 1, 0)], dimension_numbers=('NCH', 'OIH', 'NCH'), feature_group_count=E)
            xc = _silu(xc.transpose(0, 2, 1) + conv_b)
            x_dbl = xc @ W_xp.T
            dt_lo, Bm, Cm = (x_dbl[..., :R], x_dbl[..., R:R + N], x_dbl[..., R + N:])
            dt = jax.nn.softplus(dt_lo @ W_dt.T + dt_b)
            A = -jnp.exp(A_log)

            def step(h, inp):
                xt, dtt, Bt, Ct = inp
                dA = jnp.exp(dtt[:, :, None] * A)
                h = dA * h + (dtt * xt)[:, :, None] * Bt[:, None, :]
                y = jnp.einsum('ben,bn->be', h, Ct)
                return (h, y)
            h0 = jnp.zeros((Bsz, E, N), x.dtype)
            xs = (xc.transpose(1, 0, 2), dt.transpose(1, 0, 2), Bm.transpose(1, 0, 2), Cm.transpose(1, 0, 2))
            _, ys = jax.lax.scan(step, h0, xs)
            y = ys.transpose(1, 0, 2) + xc * Dp
            y = y * _silu(z)
            return y @ W_out.T
        key = jax.random.key(seed)
        ks = jax.random.split(key, 20)
        s_in = 0.02

        def mamba_params(k):
            kk = jax.random.split(k, 8)
            a_init = jnp.log(jnp.broadcast_to(jnp.arange(1, N + 1, dtype=jnp.float32), (E, N)))
            return dict(W_in=jax.random.normal(kk[0], (2 * E, D), jnp.float32) * s_in, conv_w=jax.random.normal(kk[1], (E, K), jnp.float32) * 0.1, conv_b=jnp.zeros((E,), jnp.float32), W_xp=jax.random.normal(kk[2], (R + 2 * N, E), jnp.float32) * s_in, W_dt=jax.random.normal(kk[3], (E, R), jnp.float32) * 0.1, dt_b=jnp.log(jnp.expm1(jax.random.uniform(kk[4], (E,), jnp.float32, 0.001, 0.1))), A_log=a_init, D=jnp.ones((E,), jnp.float32), W_out=jax.random.normal(kk[5], (D, E), jnp.float32) * s_in)
        p1 = mamba_params(ks[1])
        p2 = mamba_params(ks[2])
        inp = {'x': jax.random.normal(ks[0], (BATCH, L, D), jnp.float32), 'ln1_w': jnp.ones((D,), jnp.float32), 'ln1_b': jnp.zeros((D,), jnp.float32), 'ln2_w': jnp.ones((D,), jnp.float32), 'ln2_b': jnp.zeros((D,), jnp.float32)}
        for pre, p in (('m1_', p1), ('m2_', p2)):
            for k2, v in p.items():
                inp[pre + k2] = v
        return inp
    _L0_attn_in = _L0_attn_setup()

    def _L0_ffn_setup():
        import jax, jax.numpy as jnp
        import numpy as np
        D_IN, D_HID = (256, 1024)

        def _ternary(key, shape):
            return jax.random.randint(key, shape, -1, 2).astype(jnp.float32)

        def _tlin(x, w, s):
            return jnp.einsum('bsi,oi->bso', x, w) * s
        key = jax.random.key(seed)
        ks = jax.random.split(key, 12)
        inv = lambda fan: 1.0 / np.sqrt(fan).astype(np.float32)
        return {'x': jax.random.normal(ks[0], (4, 512, D_IN), dtype=jnp.float32), 'w1_w': _ternary(ks[1], (D_HID, D_IN)), 'w1_s': jax.random.uniform(ks[2], (D_HID,), dtype=jnp.float32) * inv(D_IN), 'w2_w': _ternary(ks[3], (D_HID, D_IN)), 'w2_s': jax.random.uniform(ks[4], (D_HID,), dtype=jnp.float32) * inv(D_IN), 'h1_w': _ternary(ks[5], (D_HID, D_HID)), 'h1_s': jax.random.uniform(ks[6], (D_HID,), dtype=jnp.float32) * inv(D_HID), 'h2_w': _ternary(ks[7], (D_HID, D_HID)), 'h2_s': jax.random.uniform(ks[8], (D_HID,), dtype=jnp.float32) * inv(D_HID), 'w3_w': _ternary(ks[9], (D_IN, D_HID)), 'w3_s': jax.random.uniform(ks[10], (D_IN,), dtype=jnp.float32) * inv(D_HID)}
    _L0_ffn_in = _L0_ffn_setup()
    _L0_c = _w((lambda *s: np.random.randn(*s).astype(np.float32) * 0.05)(16, 256))
    _L0_wmod = _w((lambda *s: np.random.randn(*s).astype(np.float32) * 0.05)(256, 6 * 256) * 256 ** (-0.5))
    _d = {'L0_attn_x': _L0_attn_in['x'], 'L0_attn_ln1_w': _L0_attn_in['ln1_w'], 'L0_attn_ln1_b': _L0_attn_in['ln1_b'], 'L0_attn_ln2_w': _L0_attn_in['ln2_w'], 'L0_attn_ln2_b': _L0_attn_in['ln2_b'], 'L0_attn_m1_W_in': _L0_attn_in['m1_W_in'], 'L0_attn_m1_conv_w': _L0_attn_in['m1_conv_w'], 'L0_attn_m1_conv_b': _L0_attn_in['m1_conv_b'], 'L0_attn_m1_W_xp': _L0_attn_in['m1_W_xp'], 'L0_attn_m1_W_dt': _L0_attn_in['m1_W_dt'], 'L0_attn_m1_dt_b': _L0_attn_in['m1_dt_b'], 'L0_attn_m1_A_log': _L0_attn_in['m1_A_log'], 'L0_attn_m1_D': _L0_attn_in['m1_D'], 'L0_attn_m1_W_out': _L0_attn_in['m1_W_out'], 'L0_attn_m2_W_in': _L0_attn_in['m2_W_in'], 'L0_attn_m2_conv_w': _L0_attn_in['m2_conv_w'], 'L0_attn_m2_conv_b': _L0_attn_in['m2_conv_b'], 'L0_attn_m2_W_xp': _L0_attn_in['m2_W_xp'], 'L0_attn_m2_W_dt': _L0_attn_in['m2_W_dt'], 'L0_attn_m2_dt_b': _L0_attn_in['m2_dt_b'], 'L0_attn_m2_A_log': _L0_attn_in['m2_A_log'], 'L0_attn_m2_D': _L0_attn_in['m2_D'], 'L0_attn_m2_W_out': _L0_attn_in['m2_W_out'], 'L0_ffn_w1_w': _L0_ffn_in['w1_w'], 'L0_ffn_w1_s': _L0_ffn_in['w1_s'], 'L0_ffn_w2_w': _L0_ffn_in['w2_w'], 'L0_ffn_w2_s': _L0_ffn_in['w2_s'], 'L0_ffn_h1_w': _L0_ffn_in['h1_w'], 'L0_ffn_h1_s': _L0_ffn_in['h1_s'], 'L0_ffn_h2_w': _L0_ffn_in['h2_w'], 'L0_ffn_h2_s': _L0_ffn_in['h2_s'], 'L0_ffn_w3_w': _L0_ffn_in['w3_w'], 'L0_ffn_w3_s': _L0_ffn_in['w3_s'], 'L0_c': _L0_c, 'L0_wmod': _L0_wmod}
    _x0 = _d['L0_attn_x']
    _d['L0_attn_x'] = jax.random.normal(jax.random.fold_in(jax.random.key(seed), 1), (16, 512, 256), dtype=_x0.dtype)
    del _x0
    return _d

def reference(L0_attn_x, L0_attn_ln1_w, L0_attn_ln1_b, L0_attn_ln2_w, L0_attn_ln2_b, L0_attn_m1_W_in, L0_attn_m1_conv_w, L0_attn_m1_conv_b, L0_attn_m1_W_xp, L0_attn_m1_W_dt, L0_attn_m1_dt_b, L0_attn_m1_A_log, L0_attn_m1_D, L0_attn_m1_W_out, L0_attn_m2_W_in, L0_attn_m2_conv_w, L0_attn_m2_conv_b, L0_attn_m2_W_xp, L0_attn_m2_W_dt, L0_attn_m2_dt_b, L0_attn_m2_A_log, L0_attn_m2_D, L0_attn_m2_W_out, L0_ffn_w1_w, L0_ffn_w1_s, L0_ffn_w2_w, L0_ffn_w2_s, L0_ffn_h1_w, L0_ffn_h1_s, L0_ffn_h2_w, L0_ffn_h2_s, L0_ffn_w3_w, L0_ffn_w3_s, L0_c, L0_wmod):

    def _L0_attn_ref(x, ln1_w, ln1_b, ln2_w, ln2_b, m1_W_in, m1_conv_w, m1_conv_b, m1_W_xp, m1_W_dt, m1_dt_b, m1_A_log, m1_D, m1_W_out, m2_W_in, m2_conv_w, m2_conv_b, m2_W_xp, m2_W_dt, m2_dt_b, m2_A_log, m2_D, m2_W_out):
        import jax, jax.numpy as jnp
        import numpy as np
        D = 256
        E = 2 * D
        N = 64
        R = D // 16
        K = 4
        BATCH, L = (2, 512)
        LN_EPS = 1e-05

        def _layernorm(x, w, b):
            mu = x.mean(-1, keepdims=True)
            var = ((x - mu) ** 2).mean(-1, keepdims=True)
            return (x - mu) * jax.lax.rsqrt(var + LN_EPS) * w + b

        def _silu(x):
            return x * jax.nn.sigmoid(x)

        def _mamba(x, W_in, conv_w, conv_b, W_xp, W_dt, dt_b, A_log, Dp, W_out):
            Bsz = x.shape[0]
            xz = x @ W_in.T
            xp, z = jnp.split(xz, 2, axis=-1)
            xc = jax.lax.conv_general_dilated(xp.transpose(0, 2, 1), conv_w[:, None, :], window_strides=(1,), padding=[(K - 1, 0)], dimension_numbers=('NCH', 'OIH', 'NCH'), feature_group_count=E)
            xc = _silu(xc.transpose(0, 2, 1) + conv_b)
            x_dbl = xc @ W_xp.T
            dt_lo, Bm, Cm = (x_dbl[..., :R], x_dbl[..., R:R + N], x_dbl[..., R + N:])
            dt = jax.nn.softplus(dt_lo @ W_dt.T + dt_b)
            A = -jnp.exp(A_log)

            def step(h, inp):
                xt, dtt, Bt, Ct = inp
                dA = jnp.exp(dtt[:, :, None] * A)
                h = dA * h + (dtt * xt)[:, :, None] * Bt[:, None, :]
                y = jnp.einsum('ben,bn->be', h, Ct)
                return (h, y)
            h0 = jnp.zeros((Bsz, E, N), x.dtype)
            xs = (xc.transpose(1, 0, 2), dt.transpose(1, 0, 2), Bm.transpose(1, 0, 2), Cm.transpose(1, 0, 2))
            _, ys = jax.lax.scan(step, h0, xs)
            y = ys.transpose(1, 0, 2) + xc * Dp
            y = y * _silu(z)
            return y @ W_out.T
        xn = _layernorm(x, ln1_w, ln1_b)
        x1 = _mamba(xn, m1_W_in, m1_conv_w, m1_conv_b, m1_W_xp, m1_W_dt, m1_dt_b, m1_A_log, m1_D, m1_W_out)
        xr = jnp.flip(xn, axis=1)
        x2 = jnp.flip(_mamba(xr, m2_W_in, m2_conv_w, m2_conv_b, m2_W_xp, m2_W_dt, m2_dt_b, m2_A_log, m2_D, m2_W_out), axis=1)
        x_mamba = _layernorm(x1 + x2, ln2_w, ln2_b)
        return x_mamba + xn

    def _L0_ffn_ref(x, w1_w, w1_s, w2_w, w2_s, h1_w, h1_s, h2_w, h2_s, w3_w, w3_s):
        import jax, jax.numpy as jnp
        import numpy as np
        D_IN, D_HID = (256, 1024)

        def _ternary(key, shape):
            return jax.random.randint(key, shape, -1, 2).astype(jnp.float32)

        def _tlin(x, w, s):
            return jnp.einsum('bsi,oi->bso', x, w) * s
        h = jax.nn.silu(_tlin(x, w1_w, w1_s)) * _tlin(x, w2_w, w2_s)
        h = jax.nn.gelu(_tlin(h, h1_w, h1_s), approximate=False)
        h = jax.nn.gelu(_tlin(h, h2_w, h2_s), approximate=False)
        return _tlin(h, w3_w, w3_s)
    x = L0_attn_x
    mod = (_silu(L0_c) @ L0_wmod).reshape(L0_c.shape[0], 6, 1, -1)
    sa, ca, ga, sb, cb, gb = (mod[:, 0], mod[:, 1], mod[:, 2], mod[:, 3], mod[:, 4], mod[:, 5])
    ga = (2 * (ga >= 0) - 1) * jnp.maximum(jnp.abs(ga), 0.25)
    gb = (2 * (gb >= 0) - 1) * jnp.maximum(jnp.abs(gb), 0.25)
    h = _layernorm(x, axis=-1) * (1 + ca) + sa
    x = x + ga * _L0_attn_ref(h, L0_attn_ln1_w, L0_attn_ln1_b, L0_attn_ln2_w, L0_attn_ln2_b, L0_attn_m1_W_in, L0_attn_m1_conv_w, L0_attn_m1_conv_b, L0_attn_m1_W_xp, L0_attn_m1_W_dt, L0_attn_m1_dt_b, L0_attn_m1_A_log, L0_attn_m1_D, L0_attn_m1_W_out, L0_attn_m2_W_in, L0_attn_m2_conv_w, L0_attn_m2_conv_b, L0_attn_m2_W_xp, L0_attn_m2_W_dt, L0_attn_m2_dt_b, L0_attn_m2_A_log, L0_attn_m2_D, L0_attn_m2_W_out)
    h = _layernorm(x, axis=-1) * (1 + cb) + sb
    x = x + gb * _L0_ffn_ref(h, L0_ffn_w1_w, L0_ffn_w1_s, L0_ffn_w2_w, L0_ffn_w2_s, L0_ffn_h1_w, L0_ffn_h1_s, L0_ffn_h2_w, L0_ffn_h2_s, L0_ffn_w3_w, L0_ffn_w3_s)
    return x

_drawn_inputs = setup_inputs


def setup_inputs(seed=0):
    import zlib

    import numpy as np

    out = dict(_drawn_inputs(seed))
    spreads = {'L0_attn_ln1_w': (1.0, 0.2),
     'L0_attn_ln1_b': (0.0, 0.1),
     'L0_attn_ln2_w': (1.0, 0.2),
     'L0_attn_ln2_b': (0.0, 0.1),
     'L0_attn_m1_conv_b': (0.0, 0.1),
     'L0_attn_m1_D': (1.0, 0.2),
     'L0_attn_m2_conv_b': (0.0, 0.1),
     'L0_attn_m2_D': (1.0, 0.2)}
    factors = {}
    for name, (base, spread) in spreads.items():
        noise = np.random.default_rng([zlib.crc32(name.encode()), seed]).standard_normal(out[name].shape)
        drawn = base * np.exp(spread * noise) if base else spread * noise
        out[name] = jnp.asarray(drawn.astype(out[name].dtype))
    for name, factor in factors.items():
        out[name] = (out[name] * factor).astype(out[name].dtype)
    return out
```

```python
from contextlib import ExitStack

import concourse.bass as bass
from concourse import mybir

F32 = mybir.dt.float32
F32R = mybir.dt.float32r
ALU = mybir.AluOpType
ACT = mybir.ActivationFunctionType

P = 128
BATCH, T, D = 16, 512, 256
E = 2 * D
N = 64
RANK = D // 16
HID = 1024
TAPS = 4
EPS = 1e-5
EC = E // P
DC = D // P
HC = HID // P
TT = T // P
PAD = TAPS - 1
UNITS = 2 * N
HALVES = 2 * UNITS
DECAY_RING, STATE_RING, READ_RING, C_RING = 3, 4, 2, 2

KIND_PARTS = {
    "pre": ("next",),
    "first": ("o0", "p1", "next"),
    "mid": ("early", "o0", "late", "p1", "next"),
    "last": ("early", "o0", "late", "p1"),
    "tail": ("early", "late"),
}
SCAN_PARTS = ("first", "mid", "last")


def projection_steps(part, s):
    pe = [(s, part, "T0", 1), (s + 1, part, "T1", 1)]
    act = [(s, part, "T0", 1), (s + 1, part, "T1", 1)]
    dve = []
    for m in range(EC):
        pe.append((s + 2 + 2 * m, part, f"X{m}", 1))
        act.append((s + 2 + 2 * m, part, f"X{m}", 1))
        dve.append((s + 3 + 2 * m, part, f"conv{m}", TAPS))
    act.append((s + 11, part, "xc", 1))
    for i, name in enumerate(("B", "C")):
        pe += [(s + 12 + 3 * i, part, name, 0), (s + 13 + 3 * i, part, name, 1)]
        act.append((s + 13 + 3 * i, part, name, 1))
        dve.append((s + 14 + 3 * i, part, name, 1))
    pe += [(s + 18, part, "L", 0), (s + 19, part, "L", 1)]
    act.append((s + 19, part, "L", 1))
    for m in range(EC):
        pe.append((s + 21 + m, part, f"D{m}", 1))
        act.append((s + 21 + m, part, f"D{m}", 1))
    act += [(s + 26, part, "abs", 1), (s + 27, part, "exp", 1), (s + 28, part, "one", 1)]
    dve.append((s + 30, part, "rest", 1))
    act.append((s + 31, part, "ln", 1))
    dve += [(s + 33, part, "log1p", 1), (s + 34, part, "dt", 1), (s + 35, part, "u", 1)]
    for m in range(EC):
        pe.append((s + 37 + 2 * m, part, f"Z{m}", 1))
        act.append((s + 37 + 2 * m, part, f"Z{m}", 1))
    act.append((s + 45, part, "sz", 1))
    return pe, act, dve


def side_steps():
    pe_p, act, dve, pe_q = [], [], [], []
    dve.append((0, "early", "Y1", EC + 1))
    for i, name in enumerate(("O1a", "O1b")):
        pe_q += [(1 + 2 * i, "early", name, 0), (2 + 2 * i, "early", name, 1)]
        dve.append((2 + 2 * i, "early", name, 1))
    dve.append((5, "early", "o_stats", 2 * TT))
    act.append((6, "early", "o_rstd", 2))
    dve += [(7, "early", "o_norm", 4 + TT + 2), (8, "early", "x_new", 3), (9, "early", "n_stats", 2 * TT)]
    act.append((10, "early", "n_rstd", 2))
    dve.append((11, "early", "n_norm", 4 + TT + 2))
    for k in range(DC):
        pe_q.append((12 + k, "early", f"N{k}", 1))
        act.append((12 + k, "early", f"N{k}", 1))
    for j in range(2 * HC):
        pe_q.append((14 + j, "early", f"F{j}", 1))
        act.append((14 + j, "early", f"F{j}", 1))
    act.append((30, "early", "silu", 1))
    dve += [(31, "early", "glu0", 1), (32, "early", "glu1", 1)]
    for m in range(HC):
        pe_q += [(33 + 4 * m + i, "early", f"H{m}", i // 3) for i in range(4)]
        act.append((36 + 4 * m, "early", f"H{m}", 1))
    act.append((65, "early", "gelu1", 1))
    dve.append((64, "o0", "Y0", EC + 1))
    for i, name in enumerate(("O0a", "O0b")):
        pe_q += [(66 + 2 * i, "o0", name, 0), (67 + 2 * i, "o0", name, 1)]
        act.append((67 + 2 * i, "o0", name, 1))
    for m in range(HC):
        pe_q += [(70 + 4 * m + i, "late", f"G{m}", i // 3) for i in range(4)]
        act.append((73 + 4 * m, "late", f"G{m}", 1))
    act.append((102, "late", "gelu2", 1))
    dve.append((103, "late", "gb", 1))
    for i in range(2):
        pe_q += [(104 + 4 * i + j, "late", f"W{i}", j // 3) for j in range(4)]
        dve.append((107 + 4 * i, "late", f"W{i}", 2))
    dve.append((66, "next", "x_stats", 2 * TT))
    act.append((67, "next", "x_rstd", 2))
    dve += [(68, "next", "h_norm", 4 + TT + 2), (69, "next", "h_stats", 2 * TT)]
    act.append((70, "next", "h_rstd", 2))
    dve.append((71, "next", "xn_norm", 4 + TT + 2))
    for part, s in (("p1", 4), ("next", 74)):
        a, b, c = projection_steps(part, s)
        pe_p += a
        act += b
        dve += c
    in_order = lambda steps: sorted(steps, key=lambda x: x[0])
    return in_order(pe_p), in_order(pe_q), in_order(act), in_order(dve)


PE_P, PE_Q, ACT_SIDE, DVE_SIDE = side_steps()
PE_STEPS = sorted([(*x, "p") for x in PE_P] + [(*x, "q") for x in PE_Q], key=lambda x: x[0])

CHUNKS = ([(0, "early", "O1", "O1b")] + [((1, 5, 18, 22)[c], "early", f"F{c}", f"F{4 * c + 3}") for c in range(4)]
          + [(max(26 + 4 * m, 29 + 4 * m if m > 1 else 0), "early", f"H{m}", f"H{m}") for m in range(HC)]
          + [(61, "o0", "O0", "O0b")] + [(66 + 4 * m, "late", f"G{m}", f"G{m}") for m in range(HC)]
          + [(98, "late", "W0", "W1"), (102, "late", "W1", "W1")])


class At:

    def __init__(self, b, kind):
        self.b, self.kind = b, kind

    def has(self, part):
        return part in KIND_PARTS[self.kind]


class Signal:

    def __init__(self, sem, steps, by=1):
        self.sem, self.by = sem, by
        self.steps = steps
        self.total = {k: sum(n for _, part, _, n in steps if part in parts) for k, parts in KIND_PARTS.items()}

    def before(self, at):
        t = self.total
        ahead = {"pre": 0, "first": t["pre"], "mid": t["pre"] + t["first"],
                 "last": t["pre"] + t["first"] + (BATCH - 2) * t["mid"]}
        ahead["tail"] = ahead["last"] + t["last"]
        if at.kind == "mid":
            return (at.b - 1) * (t["mid"] * self.by) + ahead["mid"] * self.by
        return ahead[at.kind] * self.by

    def done(self, at, part, name, k=None):
        count = 0
        for _, p, n, ops in self.steps:
            if p not in KIND_PARTS[at.kind]:
                continue
            if (p, n) == (part, name) and ops:
                return self.before(at) + self.by * (count + (ops if k is None else k + 1))
            count += ops
        raise KeyError((part, name))


def adaln_kernel(nc, x, win, wxp, wdt, wout, f1, h1, h2, w3, cols, rows, c_t, wmod, consts, out):
    ctx = ExitStack()
    with ctx:
        def sb(name, shape, dt=F32):
            return ctx.enter_context(nc.sbuf_tensor(name, shape, dt))

        def sem(name):
            return ctx.enter_context(nc.semaphore(name))

        mod_dram = nc.dram_tensor("mod_rows", (BATCH, 6, D), F32, kind="Internal").ap()
        xn_dram = nc.dram_tensor("xn_rows", (BATCH, T, D), F32, kind="Internal").ap()

        wxp_sb = sb("wxp_sb", [P, 2, EC, RANK + 4 * N])
        cols_sb = sb("cols_sb", [P, 2 * EC * N + 2 * EC * TAPS + 3 * 2 * EC + 4 * HC])
        o = 2 * EC * N
        a_neg = cols_sb[:, 0:o].rearrange("p (d c n) -> p d c n", d=2, c=EC)
        taps = cols_sb[:, o:o + 2 * EC * TAPS].rearrange("p (d c k) -> p d c k", d=2, c=EC)
        o += 2 * EC * TAPS
        conv_b, dt_b, d_skip = (cols_sb[:, o + 2 * EC * i:o + 2 * EC * (i + 1)].rearrange("p (d c) -> p d c", d=2)
                                for i in range(3))
        o += 3 * 2 * EC
        scales = cols_sb[:, o:o + 4 * HC].rearrange("p (s c) -> p s c", s=4)
        rows_sb = sb("rows_sb", [P, 5, D])
        ln1w, ln1b, ln2w, ln2b, w3s = (rows_sb[:, i, :] for i in range(5))
        consts_sb = sb("consts_sb", [P, 2 * P + N])
        ident, anti = consts_sb[:, 0:P], consts_sb[:, P:2 * P]
        onehot = sb("onehot", [P, N], F32R)
        eps, one = sb("eps", [P, 1]), sb("one", [P, 1])
        mod_p = sb("mod_p", [P, 2, D])
        mod_q = sb("mod_q", [P, 4, D])
        wp_sb = sb("wp_sb", [P, EC, DC, P])
        wq_sb = sb("wq_sb", [P, 2, 1024])

        decay = sb("decay", [P, DECAY_RING, 2, T])
        state = sb("state", [P, STATE_RING, 2, T])
        read = sb("read", [P, READ_RING, 2, T])
        c_row = sb("c_row", [P, C_RING, T])

        dt_sb = [sb(f"dt{d}", [P, EC, T]) for d in range(2)]
        xc_sb = [sb(f"xc{d}", [P, EC, T]) for d in range(2)]
        sz_sb = [sb(f"sz{d}", [P, EC, T]) for d in range(2)]
        u_pad = [sb(f"u{d}", [P, EC, PAD + T + 1]) for d in range(2)]
        u_sb = [u[:, :, PAD:PAD + T] for u in u_pad]
        b_parts = [sb(f"b_parts{d}", [P, T], F32R) for d in range(2)]
        c_parts = [sb(f"c_parts{d}", [P, T], F32R) for d in range(2)]

        xa = sb("xa", [P, TT, D])
        x_t = sb("x_t", [P, DC, T])
        o_sb = sb("o_sb", [P, TT, D])
        xn_q = sb("xn_q", [P, TT, D])
        x_q = sb("x_q", [P, TT, D])
        n_t = sb("n_t", [P, DC, T])
        hid1 = sb("hid1", [P, HC, T])
        hid2 = sb("hid2", [P, HC, T])
        stats = sb("stats", [P, 2, TT, 6])
        mv = sb("mv", [P, 2, TT, 2])
        ln_v = sb("ln_v", [P, 2, TT])
        rstd = sb("rstd", [P, 2, TT])
        newton = sb("newton", [P, 2, TT])
        wdt_sb = [sz[0:RANK, 1, :] for sz in sz_sb]
        dt_low = [sz[0:RANK, 0, :] for sz in sz_sb]
        wmod_sb = hid1[:, 0:6, :].rearrange("p (k a) t -> p k (a t)", k=DC)
        silu_c = sb("silu_c", [P, DC, BATCH])
        mod_sb = hid2[0:BATCH, 0:3, :].rearrange("p a t -> p (a t)")
        mod_a = hid2[0:BATCH, 3:6, :].rearrange("p a t -> p (a t)")

        y_ps = [ctx.enter_context(nc.psum_tensor(f"y_ps{c}", [P, T], F32)) for c in range(EC)]
        b_ps = ctx.enter_context(nc.psum_tensor("b_ps", [P, T], F32))
        c_ps = ctx.enter_context(nc.psum_tensor("c_ps", [P, T], F32))
        p_ps = ctx.enter_context(nc.psum_tensor("p_ps", [P, T], F32))
        q_ps = ctx.enter_context(nc.psum_tensor("q_ps", [P, T], F32))

        loaded = sem("loaded")
        setup_act, setup_dve, setup_pe, mod_stored = (sem(n) for n in ("setup_act", "setup_dve", "setup_pe",
                                                                       "mod_stored"))
        passed = sem("passed")
        b_spread, c_spread = sem("b_spread"), sem("c_spread")
        c_copied, decayed, driven, scanned, was_read, summed = (
            sem(n) for n in ("c_copied", "decayed", "driven", "scanned", "was_read", "summed"))
        pe_p = Signal(sem("pe_p"), PE_P)
        pe_q = Signal(sem("pe_q"), PE_Q)
        act_side = Signal(sem("act_side"), ACT_SIDE)
        dve_side = Signal(sem("dve_side"), DVE_SIDE)
        x_in = Signal(sem("x_in"), [(0, "next", "x", 1)], 16)
        modp_in = Signal(sem("modp_in"), [(0, "next", "modp", 1)], 16)
        xn_out = Signal(sem("xn_out"), [(0, "next", "xn", 1)], 16)
        q_in = Signal(sem("q_in"), [(0, "early", "q", 3)], 16)
        out_stored = Signal(sem("out_stored"), [(0, "late", "out", 1)], 16)
        wp_in = Signal(sem("wp_in"), [(0, "p1", "w0", 1), (1, "p1", "w1", 1), (2, "next", "w0", 1),
                                      (3, "next", "w1", 1)], 16)
        wdt_in = Signal(sem("wdt_in"), [(0, "p1", "wdt", 1), (1, "next", "wdt", 1)], 16)
        mid_slot = {(part, name): (i + 1) % 2 for i, (_, part, name, _) in enumerate(CHUNKS)}

        def chunk_slot(at, part, name):
            if at.kind == "first":
                return 0
            if at.kind == "tail" and part == "late":
                return 1 - mid_slot[part, name]
            return mid_slot[part, name]

        class ChunkSignal:

            def __init__(self):
                self.sems = [sem("wq_in0"), sem("wq_in1")]

            def counts(self, kind):
                at = At(None, kind)
                n = [0, 0]
                for _, part, name, _ in CHUNKS:
                    if at.has(part):
                        n[chunk_slot(at, part, name)] += 1
                return n

            def loaded(self, at, part, name):
                slot, count = chunk_slot(at, part, name), 0
                for _, p, nm, _ in CHUNKS:
                    if at.has(p) and chunk_slot(at, p, nm) == slot:
                        count += 1
                    if (p, nm) == (part, name):
                        break
                first, mid, last = (self.counts(k)[slot] for k in ("first", "mid", "last"))
                if at.kind == "mid":
                    return (at.b - 1) * (16 * mid) + 16 * (first + count)
                ahead = {"first": 0, "last": first + (BATCH - 2) * mid,
                         "tail": first + (BATCH - 2) * mid + last}[at.kind]
                return 16 * (ahead + count)

        wq_in = ChunkSignal()

        def of_body(at, per_body, index):
            return at.b * per_body + index

        def chunk_view(at, part, name):
            w = wq_sb[:, chunk_slot(at, part, name), :]
            if name[0] in "OW":
                return w.rearrange("p (k n) -> p k n", k=4)
            if name[0] == "F":
                return w.rearrange("p (m w k n) -> p m w k n", m=2, w=2, k=DC)
            return w.rearrange("p (k n) -> p k n", k=HC)

        def bodies(eng, body):
            body(At(-1, "pre"))
            body(At(0, "first"))
            with eng.Fori(1, BATCH - 1) as b:
                body(At(b, "mid"))
            body(At(BATCH - 1, "last"))
            body(At(BATCH, "tail"))

        def last_unit(at):
            return UNITS if at.kind in SCAN_PARTS else 128

        block = ctx.enter_context(nc.Block())

        @block.sync
        def _(sp):
            sp.sem_inc(out_stored.sem, 16)
            sp.dma_start(cols_sb[:], cols).then_inc(loaded, 16)
            sp.dma_start(rows_sb[:], rows.partition_broadcast(P)).then_inc(loaded, 16)
            sp.dma_start(consts_sb[:], consts).then_inc(loaded, 16)
            sp.dma_start(wxp_sb[:], wxp).then_inc(loaded, 16)
            sp.dma_start(silu_c[:], c_t).then_inc(loaded, 16)
            sp.dma_start(wmod_sb, wmod).then_inc(loaded, 16)
            sp.wait_ge(setup_dve, 14)
            sp.dma_start(mod_dram.rearrange("b s d -> b (s d)"), mod_sb).then_inc(mod_stored, 16)
            sp.wait_ge(mod_stored, 16)

            def wait(s, value):
                sp.wait_ge(s, value)
                sp.sem_inc(passed, 1)

            def rows_of(t, b):
                return t[bass.ds(b, 1)].rearrange("a (tt p) d -> p (a tt) d", p=P)

            def load_wp(at, part, c):
                d = 1 if part == "p1" else 0
                if c == 0:
                    if at.kind != "pre":
                        wait(pe_p.sem, pe_p.before(at) if part == "p1" else pe_p.done(at, "p1", "Z3"))
                else:
                    wait(pe_p.sem, pe_p.done(at, part, "X3"))
                sp.dma_start(wp_sb[:], win[d, c]).then_inc(wp_in.sem, 16)

            def load_wdt(at, part):
                d = 1 if part == "p1" else 0
                wait(dve_side.sem, dve_side.done(at, part, "conv3"))
                sp.dma_start(wdt_sb[d], wdt[:, d, :]).then_inc(wdt_in.sem, 16)

            def load_chunk(at, i):
                _, part, name, _ = CHUNKS[i]
                here = [c for c in CHUNKS if at.has(c[1])]
                slot = chunk_slot(at, part, name)
                same = [c for c in here if chunk_slot(at, c[1], c[2]) == slot]
                j = [c[1:3] for c in same].index((part, name))
                if j:
                    wait(pe_q.sem, pe_q.done(at, same[j - 1][1], same[j - 1][3]))
                elif at.kind != "first":
                    wait(pe_q.sem, pe_q.before(at))
                kind, n = name[0], int(name[1:])
                src = {"O": lambda: wout[n], "F": lambda: f1[n], "H": lambda: h1[n],
                       "G": lambda: h2[n], "W": lambda: w3[n]}[kind]()
                sp.dma_start(wq_sb[:, slot, :], src).then_inc(wq_in.sems[slot], 16)

            def load_next(at):
                if at.kind != "pre":
                    wait(pe_p.sem, pe_p.done(at, "p1", "T1"))
                    wait(xn_out.sem, xn_out.before(at))
                    wait(dve_side.sem, dve_side.before(at))
                nxt = at.b + 1
                sp.dma_start(xa[:], rows_of(x, nxt)).then_inc(x_in.sem, 16)
                sp.dma_start(mod_p[:], mod_dram[bass.ds(nxt, 1), 0:2, :].rearrange("a s d -> (a s) d")
                             .partition_broadcast(P)).then_inc(modp_in.sem, 16)

            def store_xn(at):
                wait(dve_side.sem, dve_side.done(at, "next", "xn_norm"))
                sp.dma_start(rows_of(xn_dram, at.b + 1), xa[:]).then_inc(xn_out.sem, 16)

            def load_previous(at):
                wait(out_stored.sem, out_stored.before(at) + 16)
                wait(xn_out.sem, xn_out.before(at))
                prev = at.b - 1
                sp.dma_start(xn_q[:], rows_of(xn_dram, prev)).then_inc(q_in.sem, 16)
                sp.dma_start(x_q[:], rows_of(x, prev)).then_inc(q_in.sem, 16)
                sp.dma_start(mod_q[:], mod_dram[bass.ds(prev, 1), 2:6, :].rearrange("a s d -> (a s) d")
                             .partition_broadcast(P)).then_inc(q_in.sem, 16)

            def store_out(at):
                wait(dve_side.sem, dve_side.done(at, "late", "W1"))
                sp.dma_start(rows_of(out, at.b - 1), x_q[:]).then_inc(out_stored.sem, 16)

            def body(at):
                if at.has("early"):
                    load_previous(at)
                for unit in range(UNITS):
                    for i, c in enumerate(CHUNKS):
                        if c[0] == unit and at.has(c[1]):
                            load_chunk(at, i)
                    if unit == 2 and at.has("p1"):
                        load_wp(at, "p1", 0)
                    if unit == 14 and at.has("p1"):
                        load_wp(at, "p1", 1)
                        load_wdt(at, "p1")
                    if unit == 60 and at.has("next"):
                        load_next(at)
                    if unit == 72 and at.has("next"):
                        store_xn(at)
                        load_wp(at, "next", 0)
                    if unit == 84 and at.has("next"):
                        load_wp(at, "next", 1)
                        load_wdt(at, "next")
                    if unit == 112 and at.has("late"):
                        store_out(at)

            bodies(sp, body)
            wait(out_stored.sem, 16 * BATCH + 16)
            wait(xn_out.sem, 16 * BATCH)

        @block.tensor
        def _(pe):
            pe.sem_inc(summed, READ_RING)
            pe.wait_ge(loaded, 16 * 6)
            pe.wait_ge(setup_act, 1)
            for j in range(3):
                for k in range(DC):
                    mm = pe.matmul(y_ps[j][0:BATCH, :], silu_c[:, k, :], wmod_sb[:, k, j * T:(j + 1) * T],
                                   start=(k == 0), stop=(k == DC - 1))
            mm.then_inc(setup_pe, 1)
            pe.wait_ge(setup_dve, 14)
            pe.wait_ge(setup_act, 4)

            def bank_free(at, stream, part, name):
                steps = [s for s in (PE_P if stream == "p" else PE_Q) if at.has(s[1]) and s[3]]
                j = [s[1:3] for s in steps].index((part, name))
                if j:
                    p, n = steps[j - 1][1:3]
                    by_dve = n in ("B", "C", "O1a", "O1b", "W0", "W1")
                    who = dve_side if by_dve else act_side
                    pe.wait_ge(who.sem, who.done(at, p, n))
                elif at.kind not in ("pre", "first"):
                    pe.wait_ge(act_side.sem, act_side.before(at))
                    pe.wait_ge(dve_side.sem, dve_side.before(at))
                elif at.kind == "first":
                    pe.wait_ge(act_side.sem, act_side.before(at))

            def project(at, part, name, quarter):
                d = 1 if part == "p1" else 0
                if quarter == 0:
                    bank_free(at, "p", part, name)
                if name[0] == "T":
                    k = int(name[1])
                    if k == 0:
                        if part == "next":
                            pe.wait_ge(dve_side.sem, dve_side.done(at, "next", "xn_norm"))
                        else:
                            pe.wait_ge(dve_side.sem, dve_side.before(at))
                    for tt in range(TT):
                        at_t = TT - 1 - tt if d else tt
                        mm = pe.matmul(p_ps[:, at_t * P:(at_t + 1) * P], xa[:, tt, k * P:(k + 1) * P],
                                       anti if d else ident, start=True, stop=True)
                elif name[0] in "XZ":
                    m = int(name[1])
                    if m == 0:
                        pe.wait_ge(wp_in.sem, wp_in.done(at, part, "w0" if name[0] == "X" else "w1"))
                    if name == "X0":
                        pe.wait_ge(act_side.sem, act_side.done(at, part, "T1"))
                    for k in range(DC):
                        mm = pe.matmul(p_ps[:], wp_sb[:, m, k, :], x_t[:, k, :], start=(k == 0), stop=(k == DC - 1))
                elif name in "BCL":
                    if name == "B" and quarter == 0:
                        pe.wait_ge(act_side.sem, act_side.done(at, part, "xc"))
                    for k in range(2 * quarter, 2 * quarter + 2):
                        if name == "L":
                            mm = pe.matmul(p_ps[0:RANK, :], wxp_sb[:, d, k, 0:RANK], xc_sb[d][:, k, :],
                                           start=(k == 0), stop=(k == EC - 1))
                        else:
                            lo = RANK + (P if name == "C" else 0)
                            mm = pe.matmul(p_ps[:], wxp_sb[:, d, k, lo:lo + P], xc_sb[d][:, k, :], start=(k == 0), stop=(k == EC - 1))
                elif name[0] == "D":
                    m = int(name[1])
                    if m == 0:
                        pe.wait_ge(act_side.sem, act_side.done(at, part, "L"))
                        pe.wait_ge(wdt_in.sem, wdt_in.done(at, part, "wdt"))
                    mm = pe.matmul(p_ps[:], wdt_sb[d][:, m * P:(m + 1) * P], dt_low[d], start=True, stop=True)
                return mm

            def network(at, part, name, quarter):
                kind, n = name[0], name[1:]
                if quarter == 0:
                    bank_free(at, "q", part, name)
                if kind == "O":
                    d, half = int(n[0]), "ab".index(n[1])
                    if half == 0 and quarter == 0:
                        pe.wait_ge(dve_side.sem, dve_side.done(at, part, f"Y{d}"))
                        pe.wait_ge(wq_in.sems[chunk_slot(at, part, f"O{d}")], wq_in.loaded(at, part, f"O{d}"))
                    w = chunk_view(at, part, f"O{d}")
                    for k in range(EC):
                        tt = 2 * half + quarter
                        mm = pe.matmul(q_ps[:, quarter * D:(quarter + 1) * D], u_sb[d][:, k, tt * P:(tt + 1) * P],
                                       w[:, k, :], start=(k == 0), stop=(k == EC - 1))
                elif kind == "N":
                    k = int(n)
                    if k == 0:
                        pe.wait_ge(dve_side.sem, dve_side.done(at, part, "n_norm"))
                    for tt in range(TT):
                        mm = pe.matmul(q_ps[:, tt * P:(tt + 1) * P], o_sb[:, tt, k * P:(k + 1) * P], ident,
                                       start=True, stop=True)
                elif kind == "F":
                    j = int(n)
                    m, which = j // 2, j % 2
                    if j == 0:
                        pe.wait_ge(act_side.sem, act_side.done(at, part, "N1"))
                    if j % 4 == 0:
                        pe.wait_ge(wq_in.sems[chunk_slot(at, part, f"F{j // 4}")], wq_in.loaded(at, part, f"F{j // 4}"))
                    w = chunk_view(at, part, f"F{j // 4}")
                    for k in range(DC):
                        mm = pe.matmul(q_ps[:], w[:, m % 2, which, k, :], n_t[:, k, :], start=(k == 0), stop=(k == DC - 1))
                elif kind in "HG":
                    m, src = int(n), (hid1 if kind == "H" else hid2)
                    if quarter == 0:
                        if m == 0 and kind == "H":
                            pe.wait_ge(dve_side.sem, dve_side.done(at, part, "glu1"))
                        if m == 0 and kind == "G":
                            pe.wait_ge(act_side.sem, act_side.done(at, "early", "gelu1"))
                        pe.wait_ge(wq_in.sems[chunk_slot(at, part, name)], wq_in.loaded(at, part, name))
                    w = chunk_view(at, part, name)
                    for k in range(2 * quarter, 2 * quarter + 2):
                        mm = pe.matmul(q_ps[:], w[:, k, :], src[:, k, :], start=(k == 0), stop=(k == HC - 1))
                else:
                    i = int(n)
                    if i == 0 and quarter == 0:
                        pe.wait_ge(act_side.sem, act_side.done(at, part, "gelu2"))
                        for name in ("W0", "W1"):
                            pe.wait_ge(wq_in.sems[chunk_slot(at, part, name)], wq_in.loaded(at, part, name))
                    ws = [chunk_view(at, part, "W0"), chunk_view(at, part, "W1")]
                    r, tt = quarter // 2, 2 * i + quarter // 2
                    for k in range(4 * (quarter % 2), 4 * (quarter % 2) + 4):
                        mm = pe.matmul(q_ps[:, r * D:(r + 1) * D], hid1[:, k, tt * P:(tt + 1) * P],
                                       ws[k // 4][:, k % 4, :], start=(k == 0), stop=(k == HC - 1))
                return mm

            def side(at, unit):
                for s, part, name, n, stream in PE_STEPS:
                    if s != unit or not at.has(part):
                        continue
                    first = min(x[0] for x in PE_STEPS if x[1:3] == (part, name))
                    mm = (project if stream == "p" else network)(at, part, name, s - first)
                    if n:
                        mm.then_inc((pe_p if stream == "p" else pe_q).sem, 1)

            def spread(at, unit):
                d, n = unit // N, unit % N
                if n == 0:
                    if d:
                        pe.wait_ge(dve_side.sem, dve_side.done(at, "p1", "C"))
                    else:
                        pe.wait_ge(dve_side.sem, dve_side.before(at))
                pe.wait_ge(driven, of_body(at, HALVES, 2 * unit) + 1)
                pe.wait_ge(c_copied, of_body(at, UNITS, unit) + 1)
                w = onehot[:, n:n + 1].to_broadcast([P, P])
                pe.matmul(b_ps[:], w, b_parts[d][:], start=True, stop=True).then_inc(b_spread, 1)
                pe.matmul(c_ps[:], w, c_parts[d][:], start=True, stop=True).then_inc(c_spread, 1)

            def accumulate(at, q):
                unit, h = q // 2, q % 2
                d, n = unit // N, unit % N
                if n == 0 and h == 0:
                    if d:
                        pe.wait_ge(dve_side.sem, dve_side.done(at, "o0", "Y0", EC - 1))
                    elif at.kind != "first":
                        pe.wait_ge(dve_side.sem, dve_side.done(at, "early", "Y1", EC - 1))
                pe.wait_ge(was_read, of_body(at, HALVES, q + 1) + STATE_RING)
                for j in range(2):
                    mm = pe.matmul(y_ps[2 * h + j][:], ident, read[:, q % READ_RING, j, :],
                                   start=(n == 0), stop=(n == N - 1))
                mm.then_inc(summed, 1)

            def body(at):
                scans = at.kind in SCAN_PARTS
                if scans:
                    spread(at, 0)
                for unit in range(UNITS):
                    if scans and unit + 1 < UNITS:
                        spread(at, unit + 1)
                    side(at, unit)
                    if scans:
                        accumulate(at, 2 * unit)
                        accumulate(at, 2 * unit + 1)

            bodies(pe, body)

        @block.scalar
        def _(act):
            act.sem_inc(c_copied, 1)
            act.wait_ge(loaded, 16 * 6)
            act.activation(silu_c[:], silu_c[:], ACT.Silu).then_inc(setup_act, 1)
            act.activation(onehot[:], consts_sb[:, 2 * P:2 * P + N], ACT.Copy).then_inc(setup_act, 1)
            act.activation(a_neg, a_neg, ACT.Exp).then_inc(setup_act, 1)
            act.wait_ge(setup_act, 3)
            act.activation(a_neg, a_neg, ACT.Copy, scale=-1.0).then_inc(setup_act, 1)
            act.wait_ge(setup_act, 4)
            act.wait_ge(setup_dve, 14)

            def side(at, unit):
                for s, part, name, _ in ACT_SIDE:
                    if s == unit and at.has(part):
                        step(at, part, name)

            def step(at, part, name):
                done = act_side.sem

                def after_pe(signal):
                    act.wait_ge(signal.sem, signal.done(at, part, name))

                if name.endswith("rstd"):
                    i = 0 if part == "next" else 1
                    act.wait_ge(dve_side.sem, dve_side.done(at, part, name[0] + "_stats"))
                    act.activation(ln_v[:, i, :], mv[:, i, :, 1], ACT.Ln, bias=eps[:]).then_inc(done, 1)
                    act.wait_ge(done, act_side.done(at, part, name, 0))
                    act.activation(rstd[:, i, :], ln_v[:, i, :], ACT.Exp, scale=-0.5).then_inc(done, 1)
                elif part in ("p1", "next"):
                    d = 1 if part == "p1" else 0
                    kind, m = name[0], (int(name[1]) if name[1:].isdigit() else 0)
                    if kind == "T":
                        after_pe(pe_p)
                        act.activation(x_t[:, m, :], p_ps[:], ACT.Copy).then_inc(done, 1)
                    elif kind == "X":
                        after_pe(pe_p)
                        if m == 0 and at.kind != "pre":
                            act.wait_ge(driven, of_body(at, HALVES, 0 if d else 2 * N) + 1)
                            if d == 0:
                                act.wait_ge(pe_q.sem, pe_q.done(at, "o0", "O0b"))
                            elif at.kind != "first":
                                act.wait_ge(pe_q.sem, pe_q.done(at, "early", "O1b"))
                        act.activation(u_sb[d][:, m, :], p_ps[:], ACT.Copy).then_inc(done, 1)
                    elif name == "xc":
                        act.wait_ge(dve_side.sem, dve_side.done(at, part, "conv3"))
                        act.activation(xc_sb[d][:], xc_sb[d][:], ACT.Silu).then_inc(done, 1)
                    elif name in "BC":
                        after_pe(pe_p)
                        if name == "B" and at.kind != "pre" and not (d and at.kind == "first"):
                            act.wait_ge(c_spread, of_body(at, UNITS, 0 if d else N))
                        act.activation((b_parts if name == "B" else c_parts)[d][:], p_ps[:], ACT.Copy).then_inc(done, 1)
                    elif name == "L":
                        after_pe(pe_p)
                        act.activation(dt_low[d], p_ps[0:RANK, :], ACT.Copy).then_inc(done, 1)
                    elif kind == "D":
                        after_pe(pe_p)
                        if m == 0 and at.kind != "pre" and not (d and at.kind == "first"):
                            act.wait_ge(decayed, of_body(at, HALVES, 0 if d else 2 * N))
                        act.activation(dt_sb[d][:, m, :], p_ps[:], ACT.Identity, bias=dt_b[:, d, m:m + 1]).then_inc(done, 1)
                    elif name == "abs":
                        act.wait_ge(done, act_side.done(at, part, "D3"))
                        act.wait_ge(dve_side.sem, dve_side.done(at, part, "conv3"))
                        act.activation(u_sb[d], dt_sb[d][:], ACT.Abs).then_inc(done, 1)
                    elif name == "exp":
                        act.wait_ge(done, act_side.done(at, part, "abs"))
                        act.activation(u_sb[d], u_sb[d], ACT.Exp, scale=-1.0).then_inc(done, 1)
                    elif name == "one":
                        act.wait_ge(done, act_side.done(at, part, "exp"))
                        act.activation(sz_sb[d][:], u_sb[d], ACT.Identity, bias=one[:]).then_inc(done, 1)
                    elif name == "ln":
                        act.wait_ge(dve_side.sem, dve_side.done(at, part, "rest"))
                        act.activation(sz_sb[d][:], sz_sb[d][:], ACT.Ln).then_inc(done, 1)
                    elif kind == "Z":
                        after_pe(pe_p)
                        if m == 0:
                            act.wait_ge(dve_side.sem, dve_side.done(at, part, "dt"))
                        act.activation(sz_sb[d][:, m, :], p_ps[:], ACT.Copy).then_inc(done, 1)
                    else:
                        act.wait_ge(done, act_side.done(at, part, "Z3"))
                        act.activation(sz_sb[d][:], sz_sb[d][:], ACT.Silu).then_inc(done, 1)
                elif name[0] == "N":
                    after_pe(pe_q)
                    act.activation(n_t[:, int(name[1]), :], q_ps[:], ACT.Copy).then_inc(done, 1)
                elif name[0] == "F":
                    after_pe(pe_q)
                    j = int(name[1:])
                    act.activation((hid2 if j % 2 else hid1)[:, j // 2, :], q_ps[:], ACT.Identity,
                                   scale=scales[:, j % 2, j // 2:j // 2 + 1]).then_inc(done, 1)
                elif name == "silu":
                    act.wait_ge(done, act_side.done(at, part, f"F{2 * HC - 1}"))
                    act.activation(hid1[:], hid1[:], ACT.Silu).then_inc(done, 1)
                elif name[0] in "HG":
                    after_pe(pe_q)
                    m, s = int(name[1]), 2 if name[0] == "H" else 3
                    if name == "H0":
                        act.wait_ge(dve_side.sem, dve_side.done(at, part, "glu1"))
                    act.activation((hid2 if s == 2 else hid1)[:, m, :], q_ps[:], ACT.Identity,
                                   scale=scales[:, s, m:m + 1]).then_inc(done, 1)
                elif name == "gelu1":
                    act.wait_ge(done, act_side.done(at, part, "H7"))
                    act.activation(hid2[:], hid2[:], ACT.Gelu).then_inc(done, 1)
                elif name == "gelu2":
                    act.wait_ge(done, act_side.done(at, part, "G7"))
                    act.activation(hid1[:], hid1[:], ACT.Gelu).then_inc(done, 1)
                else:
                    after_pe(pe_q)
                    i = "ab".index(name[2])
                    if i == 0 and at.kind != "first":
                        act.wait_ge(pe_q.sem, pe_q.done(at, "early", "N1"))
                    act.activation(o_sb[:, 2 * i:2 * i + 2, :], q_ps[:].rearrange("p (a n) -> p a n", a=2),
                                   ACT.Copy).then_inc(done, 1)

            def copy_c(at, unit):
                act.wait_ge(c_spread, of_body(at, UNITS, unit + 1))
                act.wait_ge(was_read, of_body(at, HALVES, 2 * unit + 2 - 2 * C_RING) + STATE_RING)
                act.activation(c_row[:, unit % C_RING, :], c_ps[:], ACT.Copy).then_inc(c_copied, 1)

            def decays(at, unit):
                d, n = unit // N, unit % N
                if n == 0:
                    if d:
                        act.wait_ge(dve_side.sem, dve_side.done(at, "p1", "dt"))
                    else:
                        act.wait_ge(dve_side.sem, dve_side.before(at))
                for h in range(2):
                    q = 2 * unit + h
                    act.wait_ge(scanned, of_body(at, HALVES, q + 1 - DECAY_RING if q else 0) + DECAY_RING)
                    for j in range(2):
                        c = 2 * h + j
                        ins = act.activation(decay[:, q % DECAY_RING, j, 1:T], dt_sb[d][:, c, 1:T], ACT.Exp,
                                             scale=a_neg[:, d, c, n:n + 1])
                    ins.then_inc(decayed, 1)

            def body(at):
                for unit in range(UNITS):
                    if at.kind in SCAN_PARTS:
                        copy_c(at, unit)
                        decays(at, unit)
                    side(at, unit)

            bodies(act, body)

        @block.vector
        def _(dve):
            made = [0]

            def setup(ins):
                made[0] += 1
                ins.then_inc(setup_dve, 1)
                dve.wait_ge(setup_dve, made[0])

            dve.sem_inc(scanned, DECAY_RING)
            dve.sem_inc(driven, 1)
            setup(dve.memset(eps[:], EPS))
            setup(dve.memset(one[:], 1.0))
            setup(dve.memset(decay[:, :, :, 0:1], 0.0))
            for u in u_pad:
                setup(dve.memset(u[:, :, 0:PAD], 0.0))
            dve.wait_ge(loaded, 16 * 6)
            dve.wait_ge(setup_pe, 1)
            seg = mod_sb.rearrange("p (s d) -> p s d", s=6)
            seg_a = mod_a.rearrange("p (s d) -> p s d", s=6)
            for j in range(3):
                setup(dve.tensor_copy(mod_sb[:, j * T:(j + 1) * T], y_ps[j][0:BATCH, :]))
            for s in (1, 4):
                setup(dve.tensor_scalar(seg[:, s, :], seg[:, s, :], 1.0, None, ALU.add))
            g, ga = seg[:, 2:6:3, :], seg_a[:, 2:6:3, :]
            setup(dve.scalar_tensor_tensor(ga, g, -1.0, g, ALU.mult, ALU.max))
            setup(dve.tensor_scalar(ga, ga, 0.25, None, ALU.max))
            setup(dve.tensor_scalar(g, g, 0.0, 2.0, ALU.is_ge, ALU.mult))
            setup(dve.scalar_tensor_tensor(g, g, -1.0, ga, ALU.add, ALU.mult))

            def side(at, unit):
                for s, part, name, n in DVE_SIDE:
                    if s == unit and at.has(part):
                        step(at, part, name, n)

            def step(at, part, name, n_ops):
                k = [0]

                def emit(ins, settle=False):
                    ins.then_inc(dve_side.sem, 1)
                    k[0] += 1
                    if settle:
                        dve.wait_ge(dve_side.sem, dve_side.done(at, part, name, k[0] - 1))

                def norm(i, src, dst, scale, shift):
                    v, r, t = mv[:, i, :, 1], rstd[:, i, :], newton[:, i, :]
                    emit(dve.scalar_tensor_tensor(t, v, EPS, r, ALU.add, ALU.mult), True)
                    emit(dve.tensor_tensor(t, t, r, ALU.mult), True)
                    emit(dve.tensor_scalar(t, t, -0.5, 1.5, ALU.mult, ALU.add), True)
                    emit(dve.tensor_tensor(r, r, t, ALU.mult), True)
                    for tt in range(TT):
                        emit(dve.tensor_scalar(dst[:, tt, :], src[:, tt, :], mv[:, i, tt, 0:1], rstd[:, i, tt:tt + 1],
                                               ALU.subtract, ALU.mult), tt == TT - 1)
                    emit(dve.tensor_tensor(dst[:], dst[:], over_tiles(scale), ALU.mult), True)
                    emit(dve.tensor_tensor(dst[:], dst[:], over_tiles(shift), ALU.add), True)

                def over_tiles(row):
                    return row.unsqueeze(1).to_broadcast([P, TT, D])

                def statistics(i, src):
                    for tt in range(TT):
                        emit(dve.bn_stats(stats[:, i, tt, :], src[:, tt, :]), tt == TT - 1)
                    dve.sem_inc(passed, 1)
                    for tt in range(TT):
                        emit(dve.bn_aggr(mv[:, i, tt, :], stats[:, i, tt, :]), tt == TT - 1)

                if name in ("Y0", "Y1"):
                    d = int(name[1])
                    dve.wait_ge(summed, of_body(at, HALVES, 2 * N if d == 0 else 0) + READ_RING)
                    if d == 0:
                        dve.wait_ge(act_side.sem, act_side.before(at))
                    else:
                        dve.wait_ge(act_side.sem, act_side.before(at))
                    for c in range(EC):
                        emit(dve.scalar_tensor_tensor(xc_sb[d][:, c, :], xc_sb[d][:, c, :], d_skip[:, d, c:c + 1],
                                                      y_ps[c][:], ALU.mult, ALU.add), c == EC - 1)
                    dst = u_sb[d] if d == 0 else u_pad[d][:, :, PAD + T - 1:PAD - 1:-1]
                    emit(dve.tensor_tensor(dst, xc_sb[d][:], sz_sb[d][:], ALU.mult))
                elif name in ("O1a", "O1b"):
                    i = "ab".index(name[2])
                    dve.wait_ge(pe_q.sem, pe_q.done(at, part, name))
                    dst = o_sb[:, 2 * i:2 * i + 2, :]
                    emit(dve.tensor_tensor(dst, dst, q_ps[:].rearrange("p (a n) -> p a n", a=2), ALU.add), i == 1)
                elif name == "o_stats":
                    statistics(1, o_sb)
                elif name == "o_norm":
                    dve.wait_ge(act_side.sem, act_side.done(at, part, "o_rstd"))
                    norm(1, o_sb, o_sb, ln2w, ln2b)
                elif name == "x_new":
                    dve.wait_ge(q_in.sem, q_in.done(at, "early", "q"))
                    emit(dve.tensor_tensor(o_sb[:], o_sb[:], xn_q[:], ALU.add), True)
                    emit(dve.tensor_tensor(o_sb[:], o_sb[:], over_tiles(mod_q[:, 0, :]), ALU.mult), True)
                    emit(dve.tensor_tensor(x_q[:], x_q[:], o_sb[:], ALU.add), True)
                elif name == "n_stats":
                    statistics(1, x_q)
                elif name == "n_norm":
                    dve.wait_ge(act_side.sem, act_side.done(at, part, "n_rstd"))
                    norm(1, x_q, o_sb, mod_q[:, 2, :], mod_q[:, 1, :])
                elif name in ("glu0", "glu1"):
                    i = int(name[3])
                    dve.wait_ge(act_side.sem, act_side.done(at, part, "silu"))
                    h = slice(4 * i, 4 * i + 4)
                    emit(dve.tensor_tensor(hid1[:, h, :], hid1[:, h, :], hid2[:, h, :], ALU.mult))
                elif name == "gb":
                    emit(dve.tensor_tensor(mod_q[:, 3, :], mod_q[:, 3, :], w3s, ALU.mult), True)
                elif name in ("W0", "W1"):
                    i = int(name[1])
                    dve.wait_ge(pe_q.sem, pe_q.done(at, part, name))
                    tmp = hid2[:, i, :].rearrange("p (a n) -> p a n", a=2)
                    emit(dve.tensor_tensor(tmp, q_ps[:].rearrange("p (a n) -> p a n", a=2),
                                           mod_q[:, 3, :].unsqueeze(1).to_broadcast([P, 2, D]), ALU.mult), True)
                    dst = x_q[:, 2 * i:2 * i + 2, :]
                    emit(dve.tensor_tensor(dst, dst, tmp, ALU.add))
                elif name == "x_stats":
                    dve.wait_ge(x_in.sem, x_in.done(at, "next", "x"))
                    statistics(0, xa)
                elif name == "h_norm":
                    dve.wait_ge(act_side.sem, act_side.done(at, part, "x_rstd"))
                    dve.wait_ge(modp_in.sem, modp_in.done(at, "next", "modp"))
                    norm(0, xa, xa, mod_p[:, 1, :], mod_p[:, 0, :])
                elif name == "h_stats":
                    statistics(0, xa)
                elif name == "xn_norm":
                    dve.wait_ge(act_side.sem, act_side.done(at, part, "h_rstd"))
                    norm(0, xa, xa, ln1w, ln1b)
                else:
                    d = 1 if part == "p1" else 0
                    if name.startswith("conv"):
                        m = int(name[4])
                        dve.wait_ge(act_side.sem, act_side.done(at, part, f"X{m}"))
                        dst = xc_sb[d][:, m, :]
                        for i in range(TAPS):
                            src, w = u_pad[d][:, m, i:i + T], taps[:, d, m, i:i + 1]
                            if i == 0:
                                emit(dve.tensor_scalar(dst, src, w, conv_b[:, d, m:m + 1], ALU.mult, ALU.add), True)
                            else:
                                emit(dve.scalar_tensor_tensor(dst, src, w, dst, ALU.mult, ALU.add), i < TAPS - 1)
                    elif name in ("B", "C"):
                        dve.wait_ge(act_side.sem, act_side.done(at, part, name))
                        part_sb = (b_parts if name == "B" else c_parts)[d]
                        emit(dve.tensor_tensor(part_sb[N:P, :], p_ps[N:P, :], part_sb[N:P, :].bitcast(F32),
                                               ALU.subtract))
                    elif name == "rest":
                        dve.wait_ge(act_side.sem, act_side.done(at, part, "one"))
                        emit(dve.scalar_tensor_tensor(u_sb[d], sz_sb[d][:], 1.0, u_sb[d], ALU.subtract, ALU.subtract),
                             True)
                    elif name == "log1p":
                        dve.wait_ge(act_side.sem, act_side.done(at, part, "ln"))
                        emit(dve.tensor_tensor(sz_sb[d][:], sz_sb[d][:], u_sb[d], ALU.subtract), True)
                    elif name == "dt":
                        emit(dve.scalar_tensor_tensor(dt_sb[d][:], dt_sb[d][:], 0.0, sz_sb[d][:], ALU.max, ALU.add),
                             True)
                    else:
                        emit(dve.tensor_tensor(u_sb[d], dt_sb[d][:], xc_sb[d][:], ALU.mult), True)
                assert k[0] == n_ops, (name, k[0], n_ops)

            def drive(at, q):
                unit, h = q // 2, q % 2
                d = unit // N
                if q == 0:
                    dve.wait_ge(dve_side.sem, dve_side.before(at))
                elif q == 2 * N:
                    dve.wait_ge(dve_side.sem, dve_side.done(at, "p1", "u"))
                if h == 0:
                    dve.wait_ge(b_spread, of_body(at, UNITS, unit + 1))
                dve.wait_ge(was_read, of_body(at, HALVES, q + 1 - STATE_RING) + STATE_RING)
                dve.tensor_tensor(state[:, q % STATE_RING], u_sb[d][:, 2 * h:2 * h + 2, :],
                                  b_ps[:].unsqueeze(1).to_broadcast([P, 2, T]), ALU.mult).then_inc(driven, 1)

            def scan(at, q):
                dve.wait_ge(decayed, of_body(at, HALVES, q + 1))
                dve.wait_ge(driven, of_body(at, HALVES, q + 1) + 1)
                flat = state[:, q % STATE_RING].rearrange("p j t -> p (j t)")
                dve.tensor_tensor_scan(flat, decay[:, q % DECAY_RING].rearrange("p j t -> p (j t)"), flat, 0.0,
                                       ALU.mult, ALU.add).then_inc(scanned, 1)

            def body(at):
                scans = at.kind in SCAN_PARTS
                if scans:
                    drive(at, 0)
                for unit in range(UNITS):
                    if scans:
                        for q in (2 * unit, 2 * unit + 1):
                            if q + 1 < HALVES:
                                drive(at, q + 1)
                            scan(at, q)
                    side(at, unit)

            bodies(dve, body)

        @block.gpsimd
        def _(pool):
            pool.sem_inc(was_read, STATE_RING)

            def body(at):
                if at.kind not in SCAN_PARTS:
                    return
                for q in range(HALVES):
                    unit = q // 2
                    pool.wait_ge(scanned, of_body(at, HALVES, q + 1) + DECAY_RING)
                    if q % 2 == 0:
                        pool.wait_ge(c_copied, of_body(at, UNITS, unit + 1) + 1)
                    pool.wait_ge(summed, of_body(at, HALVES, q + 1 - READ_RING) + READ_RING)
                    pool.tensor_tensor(read[:, q % READ_RING], state[:, q % STATE_RING],
                                       c_row[:, unit % C_RING, :].unsqueeze(1).to_broadcast([P, 2, T]),
                                       ALU.mult).then_inc(was_read, 1)

            bodies(pool, body)


_ORDER = ["x", "win", "wxp", "wdt", "wout", "f1", "h1", "h2", "w3", "cols", "rows", "c_t", "wmod", "consts"]


def kernel(**inputs):
    import numpy as np
    import concourse.bacc as bacc
    from concourse.bass_utils import run_bass_kernel_spmd

    g = {k: np.asarray(v) for k, v in inputs.items()}
    m = lambda name: [g[f"L0_attn_m{i}_{name}"] for i in (1, 2)]
    w = lambda name: g[f"L0_ffn_{name}"]
    by_chunk = lambda a, c: a.reshape(c, P, *a.shape[1:]).swapaxes(0, 1)
    both = lambda name: np.stack([by_chunk(a, EC) for a in m(name)], 1).reshape(P, -1)
    twice = lambda a: np.concatenate([a[:RANK]] + [a[RANK:RANK + N]] * 2 + [a[RANK + N:]] * 2)
    hidden = lambda a: a.reshape(HC, P, HC, P).transpose(0, 3, 2, 1)
    ffn_in = np.stack([w("w1_w").reshape(HC, P, DC, P), w("w2_w").reshape(HC, P, DC, P)], 1)
    arrays = {
        "x": g["L0_attn_x"],
        "win": np.stack([a.reshape(2, EC, P, DC, P).transpose(0, 4, 1, 3, 2) for a in m("W_in")]),
        "wxp": np.stack([twice(a).reshape(-1, EC, P).transpose(2, 1, 0) for a in m("W_xp")], 1),
        "wdt": np.stack([a.T for a in m("W_dt")], 1),
        "wout": np.stack([a.reshape(D, EC, P).transpose(2, 1, 0).reshape(P, -1) for a in m("W_out")]),
        "f1": ffn_in.reshape(4, 2, 2, P, DC, P).transpose(0, 5, 1, 2, 4, 3).reshape(4, P, -1),
        "h1": hidden(w("h1_w")).reshape(HC, P, -1),
        "h2": hidden(w("h2_w")).reshape(HC, P, -1),
        "w3": w("w3_w").reshape(D, 2, 4, P).transpose(1, 3, 2, 0).reshape(2, P, -1),
        "cols": np.concatenate([both("A_log"), both("conv_w"), both("conv_b"), both("dt_b"), both("D")]
                               + [by_chunk(w(s), HC) for s in ("w1_s", "w2_s", "h1_s", "h2_s")], 1),
        "rows": np.stack([g["L0_attn_ln1_w"], g["L0_attn_ln1_b"], g["L0_attn_ln2_w"], g["L0_attn_ln2_b"],
                          w("w3_s")]),
        "c_t": by_chunk(g["L0_c"].T, DC),
        "wmod": by_chunk(g["L0_wmod"], DC),
        "consts": np.concatenate([np.eye(P), np.eye(P)[::-1], np.concatenate([np.eye(N)] * 2)], 1).astype(np.float32),
    }
    nc = bacc.Bacc("TRN2", target_bir_lowering=False, num_devices=1)
    data, args = {}, []
    for name in _ORDER:
        a = np.ascontiguousarray(arrays[name])
        data[f"in_{name}"] = a
        args.append(nc.dram_tensor(f"in_{name}", a.shape, mybir.dt.from_np(a.dtype), kind="ExternalInput").ap())
    out = nc.dram_tensor("out", (BATCH, T, D), F32, kind="ExternalOutput").ap()
    adaln_kernel(nc, *args, out)
    r = run_bass_kernel_spmd(nc, [data], core_ids=[0])
    return r.results[0]["out"]
```

```python
from contextlib import ExitStack

import concourse.bass as bass
from concourse import mybir

F32 = mybir.dt.float32
F32R = mybir.dt.float32r
ALU = mybir.AluOpType
ACT = mybir.ActivationFunctionType

P = 128
BATCH, T, D = 16, 512, 256
E = 2 * D
N = 64
RANK = D // 16
HID = 1024
TAPS = 4
EPS = 1e-5
EC = E // P
DC = D // P
HC = HID // P
TT = T // P
PAD = TAPS - 1
UNITS = 2 * N
HALVES = 2 * UNITS
DECAY_RING, STATE_RING, C_RING = 3, 7, 2

KIND_PARTS = {
    "pre": ("next",),
    "first": ("o0", "p1", "next"),
    "mid": ("early", "o0", "late", "p1", "next"),
    "last": ("early", "o0", "late", "p1"),
    "tail": ("early", "late"),
}
SCAN_PARTS = ("first", "mid", "last")


def projection_steps(part, s):
    pe = [(s, part, "T0", 1), (s + 1, part, "T1", 1)]
    act = [(s, part, "T0", 1), (s + 1, part, "T1", 1)]
    dve = []
    for m in range(EC):
        pe.append((s + 2 + 2 * m, part, f"X{m}", 1))
        act.append((s + 2 + 2 * m, part, f"X{m}", 1))
        dve += [(s + 3 + 2 * m + i, part, f"conv{m}{i}", TAPS // 2) for i in range(2)]
    act.append((s + 12, part, "xc", 1))
    pe += [(s + 13, part, "BC", 0), (s + 14, part, "BC", 1)]
    act.append((s + 14, part, "BC", 2))
    dve.append((s + 15, part, "BC", 2))
    pe += [(s + 16, part, "L", 0), (s + 17, part, "L", 1)]
    act.append((s + 17, part, "L", 1))
    for m in range(EC):
        pe.append((s + 19 + m, part, f"D{m}", 1))
        act.append((s + 19 + m, part, f"D{m}", 1))
    act += [(s + 23, part, "abs", 1), (s + 24, part, "exp", 1), (s + 25, part, "one", 1)]
    dve.append((s + 27, part, "rest", 1))
    act.append((s + 28, part, "ln", 1))
    dve += [(s + 30, part, "log1p", 1), (s + 31, part, "dt", 1), (s + 32, part, "u", 1)]
    for m in range(EC):
        pe.append((s + 34 + 2 * m, part, f"Z{m}", 1))
        act.append((s + 34 + 2 * m, part, f"Z{m}", 1))
    act.append((s + 42, part, "sz", 1))
    return pe, act, dve


def norm_steps(part, name, s):
    dve = [(s, part, name + "_stats", TT), (s + 1, part, name + "_aggr", TT), (s + 3, part, name + "_norm", 4 + TT),
           (s + 5, part, name + "_scale", 1), (s + 6, part, name + "_shift", 1)]
    return [(s + 2, part, name + "_rstd", 2)], dve


def side_steps():
    pe_p, act, dve, pe_q = [], [], [], []
    dve += [(0, "early", "Y1", EC), (1, "early", "gate1", 1)]
    for i, name in enumerate(("O1a", "O1b")):
        pe_q += [(2 + 2 * i, "early", name, 0), (3 + 2 * i, "early", name, 1)]
        dve.append((3 + 2 * i, "early", name, 1))
    dve += [(13 + i, "early", f"mix{i}", 1) for i in range(3)]
    for k in range(DC):
        pe_q.append((24 + k, "early", f"N{k}", 1))
        act.append((24 + k, "early", f"N{k}", 1))
    for j in range(2 * HC):
        pe_q.append((27 + j, "early", f"F{j}", 1))
        act.append((27 + j, "early", f"F{j}", 1))
    act += [(36, "early", "silu0", 1), (43, "early", "silu1", 1)]
    dve += [((38, 39, 44, 45)[i], "early", f"glu{i}", 1) for i in range(4)]
    for m in range(HC):
        pe_q += [(46 + 4 * m + i, "early", f"H{m}", i // 3) for i in range(4)]
        act.append((49 + 4 * m, "early", f"H{m}", 1))
    act += [(62, "early", "gelu0", 1), (78, "early", "gelu1", 1)]
    dve += [(64, "o0", "Y0", EC), (65, "o0", "gate0", 1)]
    for i, name in enumerate(("O0a", "O0b")):
        pe_q += [(78 + 2 * i, "o0", name, 0), (79 + 2 * i, "o0", name, 1)]
        act.append((79 + 2 * i, "o0", name, 1))
    for m in range(HC):
        pe_q += [(83 + 4 * m + i, "late", f"G{m}", i // 3) for i in range(4)]
        act.append((86 + 4 * m, "late", f"G{m}", 1))
    act += [(100, "late", "gelu2", 1), (115, "late", "gelu3", 1)]
    dve.append((115, "late", "gb", 1))
    for i in range(2):
        pe_q += [(117 + 4 * i + j, "late", f"W{i}", j // 3) for j in range(4)]
        dve.append((120 + 4 * i, "late", f"W{i}", 2))
    for part, name, s in (("early", "o", 6), ("early", "n", 16), ("next", "x", 66), ("next", "h", 73)):
        a, c = norm_steps(part, name, s)
        act += a
        dve += c
    for part, s in (("p1", 6), ("next", 81)):
        a, b, c = projection_steps(part, s)
        pe_p += a
        act += b
        dve += c
    in_order = lambda steps: sorted(steps, key=lambda x: x[0])
    return in_order(pe_p), in_order(pe_q), in_order(act), in_order(dve)


PE_P, PE_Q, ACT_SIDE, DVE_SIDE = side_steps()
PE_STEPS = sorted([(*x, "p") for x in PE_P] + [(*x, "q") for x in PE_Q], key=lambda x: x[0])

CHUNKS = ([(0, "early", "O1", "O1b")] + [((1, 6, 31, 35)[c], "early", f"F{c}", f"F{4 * c + 3}") for c in range(4)]
          + [((39, 43)[m] if m < 2 else 42 + 4 * m, "early", f"H{m}", f"H{m}") for m in range(HC)]
          + [(74, "o0", "O0", "O0b")] + [((78, 82)[m] if m < 2 else 79 + 4 * m, "late", f"G{m}", f"G{m}")
                                         for m in range(HC)]
          + [(111, "late", "W0", "W1"), (115, "late", "W1", "W1")])


class At:

    def __init__(self, b, kind):
        self.b, self.kind = b, kind

    def has(self, part):
        return part in KIND_PARTS[self.kind]


class Signal:

    def __init__(self, sem, steps, by=1):
        self.sem, self.by = sem, by
        self.steps = steps
        self.total = {k: sum(n for _, part, _, n in steps if part in parts) for k, parts in KIND_PARTS.items()}

    def before(self, at):
        t = self.total
        ahead = {"pre": 0, "first": t["pre"], "mid": t["pre"] + t["first"],
                 "last": t["pre"] + t["first"] + (BATCH - 2) * t["mid"]}
        ahead["tail"] = ahead["last"] + t["last"]
        if at.kind == "mid":
            return (at.b - 1) * (t["mid"] * self.by) + ahead["mid"] * self.by
        return ahead[at.kind] * self.by

    def done(self, at, part, name, k=None):
        count = 0
        for _, p, n, ops in self.steps:
            if p not in KIND_PARTS[at.kind]:
                continue
            if (p, n) == (part, name) and ops:
                return self.before(at) + self.by * (count + (ops if k is None else k + 1))
            count += ops
        raise KeyError((part, name))


def adaln_kernel(nc, x, win, wxp, wdt, wout, f1, h1, h2, w3, cols, rows, c_t, wmod, consts, out):
    ctx = ExitStack()
    with ctx:
        def sb(name, shape, dt=F32):
            return ctx.enter_context(nc.sbuf_tensor(name, shape, dt))

        def sem(name):
            return ctx.enter_context(nc.semaphore(name))

        mod_dram = nc.dram_tensor("mod_rows", (BATCH, 6, D), F32, kind="Internal").ap()
        xn_dram = nc.dram_tensor("xn_rows", (BATCH, T, D), F32, kind="Internal").ap()

        wxp_sb = sb("wxp_sb", [P, 2, EC, RANK + 2 * N])
        cols_sb = sb("cols_sb", [P, 2 * EC * N + 2 * EC * TAPS + 3 * 2 * EC + 4 * HC])
        o = 2 * EC * N
        a_neg = cols_sb[:, 0:o].rearrange("p (d c n) -> p d c n", d=2, c=EC)
        taps = cols_sb[:, o:o + 2 * EC * TAPS].rearrange("p (d c k) -> p d c k", d=2, c=EC)
        o += 2 * EC * TAPS
        conv_b, dt_b, d_skip = (cols_sb[:, o + 2 * EC * i:o + 2 * EC * (i + 1)].rearrange("p (d c) -> p d c", d=2)
                                for i in range(3))
        o += 3 * 2 * EC
        scales = cols_sb[:, o:o + 4 * HC].rearrange("p (s c) -> p s c", s=4)
        rows_sb = sb("rows_sb", [P, 5, D])
        ln1w, ln1b, ln2w, ln2b, w3s = (rows_sb[:, i, :] for i in range(5))
        consts_sb = sb("consts_sb", [P, 2 * P + N])
        ident, anti = consts_sb[:, 0:P], consts_sb[:, P:2 * P]
        onehot = sb("onehot", [P, N], F32R)
        eps, one = sb("eps", [P, 1]), sb("one", [P, 1])
        mod_p = sb("mod_p", [P, 2, D])
        mod_q = sb("mod_q", [P, 4, D])
        wp_sb = sb("wp_sb", [P, EC, DC, P])
        wq_sb = sb("wq_sb", [P, 2, 1024])

        decay = sb("decay", [P, DECAY_RING, 2, T])
        state = sb("state", [P, STATE_RING, 2, T])
        c_row = sb("c_row", [P, C_RING, T])

        dt_sb = [sb(f"dt{d}", [P, EC, T]) for d in range(2)]
        xc_sb = [sb(f"xc{d}", [P, EC, T]) for d in range(2)]
        sz_sb = [sb(f"sz{d}", [P, EC, T]) for d in range(2)]
        u_pad = [sb(f"u{d}", [P, EC, PAD + T + 1]) for d in range(2)]
        u_sb = [u[:, :, PAD:PAD + T] for u in u_pad]
        b_parts = [sb(f"b_parts{d}", [P, T], F32R) for d in range(2)]
        c_parts = [sb(f"c_parts{d}", [P, T], F32R) for d in range(2)]

        xa = sb("xa", [P, TT, D])
        x_t = sb("x_t", [P, DC, T])
        o_sb = sb("o_sb", [P, TT, D])
        xn_q = sb("xn_q", [P, TT, D])
        x_q = sb("x_q", [P, TT, D])
        n_t = xn_q[:].rearrange("p a d -> p (a d)").rearrange("p (k t) -> p k t", k=DC)
        hid1 = sb("hid1", [P, HC, T])
        hid2 = sb("hid2", [P, HC, T])
        stats = sb("stats", [P, 2, TT, 6])
        mv = sb("mv", [P, 2, TT, 2])
        ln_v = sb("ln_v", [P, 2, TT])
        rstd = sb("rstd", [P, 2, TT])
        newton = sb("newton", [P, 2, TT])
        wdt_sb = [sz[0:RANK, 1, :] for sz in sz_sb]
        dt_low = [sz[0:RANK, 0, :] for sz in sz_sb]
        wmod_sb = hid1[:, 0:6, :].rearrange("p (k a) t -> p k (a t)", k=DC)
        silu_c = sb("silu_c", [P, DC, BATCH])
        mod_sb = hid2[0:BATCH, 0:3, :].rearrange("p a t -> p (a t)")
        mod_a = hid2[0:BATCH, 3:6, :].rearrange("p a t -> p (a t)")

        y_ps = [ctx.enter_context(nc.psum_tensor(f"y_ps{c}", [P, T], F32)) for c in range(EC)]
        b_ps = ctx.enter_context(nc.psum_tensor("b_ps", [P, T], F32))
        c_ps = ctx.enter_context(nc.psum_tensor("c_ps", [P, T], F32))
        p_ps = ctx.enter_context(nc.psum_tensor("p_ps", [P, T], F32))
        q_ps = ctx.enter_context(nc.psum_tensor("q_ps", [P, T], F32))

        loaded = sem("loaded")
        setup_act, setup_dve, setup_pe, mod_stored = (sem(n) for n in ("setup_act", "setup_dve", "setup_pe",
                                                                       "mod_stored"))
        passed = sem("passed")
        b_spread, c_spread = sem("b_spread"), sem("c_spread")
        c_copied, decayed, driven, scanned, was_read, summed = (
            sem(n) for n in ("c_copied", "decayed", "driven", "scanned", "was_read", "summed"))
        pe_p = Signal(sem("pe_p"), PE_P)
        pe_q = Signal(sem("pe_q"), PE_Q)
        act_side = Signal(sem("act_side"), ACT_SIDE)
        dve_side = Signal(sem("dve_side"), DVE_SIDE)
        x_in = Signal(sem("x_in"), [(0, "next", "x", 1)], 16)
        modp_in = Signal(sem("modp_in"), [(0, "next", "modp", 1)], 16)
        xn_out = Signal(sem("xn_out"), [(0, "next", "xn", 1)], 16)
        q_in = Signal(sem("q_in"), [(0, "early", "q", 3)], 16)
        out_stored = Signal(sem("out_stored"), [(0, "late", "out", 1)], 16)
        wp_in = Signal(sem("wp_in"), [(0, "p1", "w0", 1), (1, "p1", "w1", 1), (2, "next", "w0", 1),
                                      (3, "next", "w1", 1)], 16)
        wdt_in = Signal(sem("wdt_in"), [(0, "p1", "wdt", 1), (1, "next", "wdt", 1)], 16)
        mid_slot = {(part, name): (i + 1) % 2 for i, (_, part, name, _) in enumerate(CHUNKS)}

        def chunk_slot(at, part, name):
            if at.kind == "first":
                return 0
            if at.kind == "tail" and part == "late":
                return 1 - mid_slot[part, name]
            return mid_slot[part, name]

        class ChunkSignal:

            def __init__(self):
                self.sems = [sem("wq_in0"), sem("wq_in1")]

            def counts(self, kind):
                at = At(None, kind)
                n = [0, 0]
                for _, part, name, _ in CHUNKS:
                    if at.has(part):
                        n[chunk_slot(at, part, name)] += 1
                return n

            def loaded(self, at, part, name):
                slot, count = chunk_slot(at, part, name), 0
                for _, p, nm, _ in CHUNKS:
                    if at.has(p) and chunk_slot(at, p, nm) == slot:
                        count += 1
                    if (p, nm) == (part, name):
                        break
                first, mid, last = (self.counts(k)[slot] for k in ("first", "mid", "last"))
                if at.kind == "mid":
                    return (at.b - 1) * (16 * mid) + 16 * (first + count)
                ahead = {"first": 0, "last": first + (BATCH - 2) * mid,
                         "tail": first + (BATCH - 2) * mid + last}[at.kind]
                return 16 * (ahead + count)

        wq_in = ChunkSignal()

        def of_body(at, per_body, index):
            return at.b * per_body + index

        def last_user(q, ring):
            if q >= ring:
                return q - ring
            return max(r for r in range(HALVES) if r % ring == q) - HALVES

        def chunk_view(at, part, name):
            w = wq_sb[:, chunk_slot(at, part, name), :]
            if name[0] in "OW":
                return w.rearrange("p (k n) -> p k n", k=4)
            if name[0] == "F":
                return w.rearrange("p (m w k n) -> p m w k n", m=2, w=2, k=DC)
            return w.rearrange("p (k n) -> p k n", k=HC)

        def bodies(eng, body):
            body(At(-1, "pre"))
            body(At(0, "first"))
            with eng.Fori(1, BATCH - 1) as b:
                body(At(b, "mid"))
            body(At(BATCH - 1, "last"))
            body(At(BATCH, "tail"))

        def last_unit(at):
            return UNITS if at.kind in SCAN_PARTS else 128

        block = ctx.enter_context(nc.Block())

        @block.sync
        def _(sp):
            sp.sem_inc(out_stored.sem, 16)
            sp.dma_start(cols_sb[:], cols).then_inc(loaded, 16)
            sp.dma_start(rows_sb[:], rows.partition_broadcast(P)).then_inc(loaded, 16)
            sp.dma_start(consts_sb[:], consts).then_inc(loaded, 16)
            sp.dma_start(wxp_sb[:], wxp).then_inc(loaded, 16)
            sp.dma_start(silu_c[:], c_t).then_inc(loaded, 16)
            sp.dma_start(wmod_sb, wmod).then_inc(loaded, 16)
            sp.wait_ge(setup_dve, 14)
            sp.dma_start(mod_dram.rearrange("b s d -> b (s d)"), mod_sb).then_inc(mod_stored, 16)
            sp.wait_ge(mod_stored, 16)

            def wait(s, value):
                sp.wait_ge(s, value)
                sp.sem_inc(passed, 1)

            def rows_of(t, b):
                return t[bass.ds(b, 1)].rearrange("a (tt p) d -> p (a tt) d", p=P)

            def load_wp(at, part, c):
                d = 1 if part == "p1" else 0
                if c == 0:
                    if at.kind != "pre":
                        wait(pe_p.sem, pe_p.before(at) if part == "p1" else pe_p.done(at, "p1", "Z3"))
                else:
                    wait(pe_p.sem, pe_p.done(at, part, "X3"))
                sp.dma_start(wp_sb[:], win[d, c]).then_inc(wp_in.sem, 16)

            def load_wdt(at, part):
                d = 1 if part == "p1" else 0
                wait(dve_side.sem, dve_side.done(at, part, "conv31"))
                sp.dma_start(wdt_sb[d], wdt[:, d, :]).then_inc(wdt_in.sem, 16)

            def load_chunk(at, i):
                _, part, name, _ = CHUNKS[i]
                here = [c for c in CHUNKS if at.has(c[1])]
                slot = chunk_slot(at, part, name)
                same = [c for c in here if chunk_slot(at, c[1], c[2]) == slot]
                j = [c[1:3] for c in same].index((part, name))
                if j:
                    wait(pe_q.sem, pe_q.done(at, same[j - 1][1], same[j - 1][3]))
                elif at.kind != "first":
                    wait(pe_q.sem, pe_q.before(at))
                kind, n = name[0], int(name[1:])
                src = {"O": lambda: wout[n], "F": lambda: f1[n], "H": lambda: h1[n],
                       "G": lambda: h2[n], "W": lambda: w3[n]}[kind]()
                sp.dma_start(wq_sb[:, slot, :], src).then_inc(wq_in.sems[slot], 16)

            def load_next(at):
                if at.kind != "pre":
                    wait(pe_p.sem, pe_p.done(at, "p1", "T1"))
                    wait(xn_out.sem, xn_out.before(at))
                    wait(dve_side.sem, dve_side.before(at))
                nxt = at.b + 1
                sp.dma_start(xa[:], rows_of(x, nxt)).then_inc(x_in.sem, 16)
                sp.dma_start(mod_p[:], mod_dram[bass.ds(nxt, 1), 0:2, :].rearrange("a s d -> (a s) d")
                             .partition_broadcast(P)).then_inc(modp_in.sem, 16)

            def store_xn(at):
                wait(dve_side.sem, dve_side.done(at, "next", "h_shift"))
                sp.dma_start(rows_of(xn_dram, at.b + 1), xa[:]).then_inc(xn_out.sem, 16)

            def load_previous(at):
                wait(out_stored.sem, out_stored.before(at) + 16)
                wait(xn_out.sem, xn_out.before(at))
                prev = at.b - 1
                sp.dma_start(xn_q[:], rows_of(xn_dram, prev)).then_inc(q_in.sem, 16)
                sp.dma_start(x_q[:], rows_of(x, prev)).then_inc(q_in.sem, 16)
                sp.dma_start(mod_q[:], mod_dram[bass.ds(prev, 1), 2:6, :].rearrange("a s d -> (a s) d")
                             .partition_broadcast(P)).then_inc(q_in.sem, 16)

            def store_out(at):
                wait(dve_side.sem, dve_side.done(at, "late", "W1"))
                sp.dma_start(rows_of(out, at.b - 1), x_q[:]).then_inc(out_stored.sem, 16)

            def body(at):
                if at.has("early"):
                    load_previous(at)
                for unit in range(UNITS):
                    for i, c in enumerate(CHUNKS):
                        if c[0] == unit and at.has(c[1]):
                            load_chunk(at, i)
                    if unit == 1 and at.has("p1"):
                        load_wp(at, "p1", 0)
                    if unit == 15 and at.has("p1"):
                        load_wp(at, "p1", 1)
                    if unit == 17 and at.has("p1"):
                        load_wdt(at, "p1")
                    if unit == 58 and at.has("next"):
                        load_next(at)
                        load_wp(at, "next", 0)
                    if unit == 80 and at.has("next"):
                        store_xn(at)
                    if unit == 90 and at.has("next"):
                        load_wp(at, "next", 1)
                    if unit == 92 and at.has("next"):
                        load_wdt(at, "next")
                    if unit == 125 and at.has("late"):
                        store_out(at)

            bodies(sp, body)
            wait(out_stored.sem, 16 * BATCH + 16)
            wait(xn_out.sem, 16 * BATCH)

        @block.tensor
        def _(pe):
            pe.sem_inc(summed, STATE_RING)
            pe.wait_ge(loaded, 16 * 6)
            pe.wait_ge(setup_act, 1)
            for j in range(3):
                for k in range(DC):
                    mm = pe.matmul(y_ps[j][0:BATCH, :], silu_c[:, k, :], wmod_sb[:, k, j * T:(j + 1) * T],
                                   start=(k == 0), stop=(k == DC - 1))
            mm.then_inc(setup_pe, 1)
            pe.wait_ge(setup_dve, 14)
            pe.wait_ge(setup_act, 4)

            def bank_free(at, stream, part, name):
                steps = [s for s in (PE_P if stream == "p" else PE_Q) if at.has(s[1]) and s[3]]
                j = [s[1:3] for s in steps].index((part, name))
                if j:
                    p, n = steps[j - 1][1:3]
                    by_dve = n in ("BC", "O1a", "O1b", "W0", "W1")
                    who = dve_side if by_dve else act_side
                    pe.wait_ge(who.sem, who.done(at, p, n))
                elif at.kind not in ("pre", "first"):
                    pe.wait_ge(act_side.sem, act_side.before(at))
                    pe.wait_ge(dve_side.sem, dve_side.before(at))
                elif at.kind == "first":
                    pe.wait_ge(act_side.sem, act_side.before(at))

            def project(at, part, name, quarter):
                d = 1 if part == "p1" else 0
                if quarter == 0:
                    bank_free(at, "p", part, name)
                if name[0] == "T":
                    k = int(name[1])
                    if k == 0:
                        if part == "next":
                            pe.wait_ge(dve_side.sem, dve_side.done(at, "next", "h_shift"))
                        else:
                            pe.wait_ge(dve_side.sem, dve_side.before(at))
                    for tt in range(TT):
                        at_t = TT - 1 - tt if d else tt
                        mm = pe.matmul(p_ps[:, at_t * P:(at_t + 1) * P], xa[:, tt, k * P:(k + 1) * P],
                                       anti if d else ident, start=True, stop=True)
                elif name[0] in "XZ":
                    m = int(name[1])
                    if m == 0:
                        pe.wait_ge(wp_in.sem, wp_in.done(at, part, "w0" if name[0] == "X" else "w1"))
                    if name == "X0":
                        pe.wait_ge(act_side.sem, act_side.done(at, part, "T1"))
                    for k in range(DC):
                        mm = pe.matmul(p_ps[:], wp_sb[:, m, k, :], x_t[:, k, :], start=(k == 0), stop=(k == DC - 1))
                elif name in ("BC", "L"):
                    if name == "BC" and quarter == 0:
                        pe.wait_ge(act_side.sem, act_side.done(at, part, "xc"))
                    for k in range(2 * quarter, 2 * quarter + 2):
                        if name == "L":
                            mm = pe.matmul(p_ps[0:RANK, :], wxp_sb[:, d, k, 0:RANK], xc_sb[d][:, k, :],
                                           start=(k == 0), stop=(k == EC - 1))
                        else:
                            mm = pe.matmul(p_ps[:], wxp_sb[:, d, k, RANK:RANK + P], xc_sb[d][:, k, :],
                                           start=(k == 0), stop=(k == EC - 1))
                elif name[0] == "D":
                    m = int(name[1])
                    if m == 0:
                        pe.wait_ge(act_side.sem, act_side.done(at, part, "L"))
                        pe.wait_ge(wdt_in.sem, wdt_in.done(at, part, "wdt"))
                    mm = pe.matmul(p_ps[:], wdt_sb[d][:, m * P:(m + 1) * P], dt_low[d], start=True, stop=True)
                return mm

            def network(at, part, name, quarter):
                kind, n = name[0], name[1:]
                if quarter == 0:
                    bank_free(at, "q", part, name)
                if kind == "O":
                    d, half = int(n[0]), "ab".index(n[1])
                    if half == 0 and quarter == 0:
                        pe.wait_ge(dve_side.sem, dve_side.done(at, part, f"gate{d}"))
                        pe.wait_ge(wq_in.sems[chunk_slot(at, part, f"O{d}")], wq_in.loaded(at, part, f"O{d}"))
                    w = chunk_view(at, part, f"O{d}")
                    for k in range(EC):
                        tt = 2 * half + quarter
                        mm = pe.matmul(q_ps[:, quarter * D:(quarter + 1) * D], u_sb[d][:, k, tt * P:(tt + 1) * P],
                                       w[:, k, :], start=(k == 0), stop=(k == EC - 1))
                elif kind == "N":
                    k = int(n)
                    if k == 0:
                        pe.wait_ge(dve_side.sem, dve_side.done(at, part, "n_shift"))
                    for tt in range(TT):
                        mm = pe.matmul(q_ps[:, tt * P:(tt + 1) * P], o_sb[:, tt, k * P:(k + 1) * P], ident,
                                       start=True, stop=True)
                elif kind == "F":
                    j = int(n)
                    m, which = j // 2, j % 2
                    if j == 0:
                        pe.wait_ge(act_side.sem, act_side.done(at, part, "N1"))
                    if j % 4 == 0:
                        pe.wait_ge(wq_in.sems[chunk_slot(at, part, f"F{j // 4}")], wq_in.loaded(at, part, f"F{j // 4}"))
                    w = chunk_view(at, part, f"F{j // 4}")
                    for k in range(DC):
                        mm = pe.matmul(q_ps[:], w[:, m % 2, which, k, :], n_t[:, k, :], start=(k == 0), stop=(k == DC - 1))
                elif kind in "HG":
                    m, src = int(n), (hid1 if kind == "H" else hid2)
                    if quarter == 0:
                        if m == 0 and kind == "H":
                            pe.wait_ge(dve_side.sem, dve_side.done(at, part, "glu3"))
                        if m == 0 and kind == "G":
                            pe.wait_ge(act_side.sem, act_side.done(at, "early", "gelu1"))
                        pe.wait_ge(wq_in.sems[chunk_slot(at, part, name)], wq_in.loaded(at, part, name))
                    w = chunk_view(at, part, name)
                    for k in range(2 * quarter, 2 * quarter + 2):
                        mm = pe.matmul(q_ps[:], w[:, k, :], src[:, k, :], start=(k == 0), stop=(k == HC - 1))
                else:
                    i = int(n)
                    if i == 0 and quarter == 0:
                        pe.wait_ge(act_side.sem, act_side.done(at, part, "gelu3"))
                        for name in ("W0", "W1"):
                            pe.wait_ge(wq_in.sems[chunk_slot(at, part, name)], wq_in.loaded(at, part, name))
                    ws = [chunk_view(at, part, "W0"), chunk_view(at, part, "W1")]
                    r, tt = quarter // 2, 2 * i + quarter // 2
                    for k in range(4 * (quarter % 2), 4 * (quarter % 2) + 4):
                        mm = pe.matmul(q_ps[:, r * D:(r + 1) * D], hid1[:, k, tt * P:(tt + 1) * P],
                                       ws[k // 4][:, k % 4, :], start=(k == 0), stop=(k == HC - 1))
                return mm

            def side(at, unit):
                for s, part, name, n, stream in PE_STEPS:
                    if s != unit or not at.has(part):
                        continue
                    first = min(x[0] for x in PE_STEPS if x[1:3] == (part, name))
                    mm = (project if stream == "p" else network)(at, part, name, s - first)
                    if n:
                        mm.then_inc((pe_p if stream == "p" else pe_q).sem, 1)

            def spread(at, unit):
                d, n = unit // N, unit % N
                if n == 0:
                    if d:
                        pe.wait_ge(dve_side.sem, dve_side.done(at, "p1", "BC"))
                    else:
                        pe.wait_ge(dve_side.sem, dve_side.before(at))
                pe.wait_ge(driven, of_body(at, HALVES, 2 * unit) + 1)
                pe.wait_ge(c_copied, of_body(at, UNITS, unit) + 1)
                w = onehot[:, n:n + 1].to_broadcast([P, P])
                pe.matmul(b_ps[:], w, b_parts[d][:], start=True, stop=True).then_inc(b_spread, 1)
                pe.matmul(c_ps[:], w, c_parts[d][:], start=True, stop=True).then_inc(c_spread, 1)

            def accumulate(at, q):
                at_q = q % HALVES
                unit, h = at_q // 2, at_q % 2
                d, n = unit // N, unit % N
                if n == 0 and h == 0:
                    if d:
                        pe.wait_ge(dve_side.sem, dve_side.done(at, "o0", "Y0", EC - 1))
                    elif at.kind != "first":
                        pe.wait_ge(dve_side.sem, dve_side.done(at, "early", "Y1", EC - 1))
                pe.wait_ge(was_read, of_body(at, HALVES, q + 1) + 2 * C_RING)
                for j in range(2):
                    mm = pe.matmul(y_ps[2 * h + j][:], ident, state[:, at_q % STATE_RING, j, :],
                                   start=(n == 0), stop=(n == N - 1))
                mm.then_inc(summed, 1)

            def body(at):
                scans = at.kind in SCAN_PARTS
                if scans:
                    spread(at, 0)
                for unit in range(UNITS):
                    behind = (2 * unit - 2, 2 * unit - 1) if unit or at.kind in ("mid", "last", "tail") else ()
                    if unit == 0:
                        for q in behind:
                            accumulate(at, q)
                    if scans and unit + 1 < UNITS:
                        spread(at, unit + 1)
                    side(at, unit)
                    if scans and unit:
                        for q in behind:
                            accumulate(at, q)

            bodies(pe, body)

        @block.scalar
        def _(act):
            act.sem_inc(c_copied, 1)
            act.wait_ge(loaded, 16 * 6)
            act.activation(silu_c[:], silu_c[:], ACT.Silu).then_inc(setup_act, 1)
            act.activation(onehot[:], consts_sb[:, 2 * P:2 * P + N], ACT.Copy).then_inc(setup_act, 1)
            act.activation(a_neg, a_neg, ACT.Exp).then_inc(setup_act, 1)
            act.wait_ge(setup_act, 3)
            act.activation(a_neg, a_neg, ACT.Copy, scale=-1.0).then_inc(setup_act, 1)
            act.wait_ge(setup_act, 4)
            act.wait_ge(setup_dve, 14)

            def side(at, unit):
                for s, part, name, _ in ACT_SIDE:
                    if s == unit and at.has(part):
                        step(at, part, name)

            def step(at, part, name):
                done = act_side.sem

                def after_pe(signal):
                    act.wait_ge(signal.sem, signal.done(at, part, name))

                if name.endswith("rstd"):
                    i = 0 if part == "next" else 1
                    act.wait_ge(dve_side.sem, dve_side.done(at, part, name[0] + "_aggr"))
                    act.activation(ln_v[:, i, :], mv[:, i, :, 1], ACT.Ln, bias=eps[:]).then_inc(done, 1)
                    act.wait_ge(done, act_side.done(at, part, name, 0))
                    act.activation(rstd[:, i, :], ln_v[:, i, :], ACT.Exp, scale=-0.5).then_inc(done, 1)
                elif part in ("p1", "next"):
                    d = 1 if part == "p1" else 0
                    kind, m = name[0], (int(name[1]) if name[1:].isdigit() else 0)
                    if kind == "T":
                        after_pe(pe_p)
                        act.activation(x_t[:, m, :], p_ps[:], ACT.Copy).then_inc(done, 1)
                    elif kind == "X":
                        after_pe(pe_p)
                        if m == 0 and at.kind != "pre":
                            act.wait_ge(driven, of_body(at, HALVES, 0 if d else 2 * N) + 1)
                            if d == 0:
                                act.wait_ge(pe_q.sem, pe_q.done(at, "o0", "O0b"))
                            elif at.kind != "first":
                                act.wait_ge(pe_q.sem, pe_q.done(at, "early", "O1b"))
                        act.activation(u_sb[d][:, m, :], p_ps[:], ACT.Copy).then_inc(done, 1)
                    elif name == "xc":
                        act.wait_ge(dve_side.sem, dve_side.done(at, part, "conv31"))
                        act.activation(xc_sb[d][:], xc_sb[d][:], ACT.Silu).then_inc(done, 1)
                    elif name == "BC":
                        after_pe(pe_p)
                        if at.kind != "pre" and not (d and at.kind == "first"):
                            act.wait_ge(c_spread, of_body(at, UNITS, 0 if d else N))
                        act.activation(b_parts[d][0:N, :], p_ps[0:N, :], ACT.Copy).then_inc(done, 1)
                        act.activation(c_parts[d][N:P, :], p_ps[N:P, :], ACT.Copy).then_inc(done, 1)
                    elif name == "L":
                        after_pe(pe_p)
                        act.activation(dt_low[d], p_ps[0:RANK, :], ACT.Copy).then_inc(done, 1)
                    elif kind == "D":
                        after_pe(pe_p)
                        if m == 0 and at.kind != "pre" and not (d and at.kind == "first"):
                            act.wait_ge(decayed, of_body(at, HALVES, 0 if d else 2 * N))
                        act.activation(dt_sb[d][:, m, :], p_ps[:], ACT.Identity, bias=dt_b[:, d, m:m + 1]).then_inc(done, 1)
                    elif name == "abs":
                        act.wait_ge(done, act_side.done(at, part, "D3"))
                        act.wait_ge(dve_side.sem, dve_side.done(at, part, "conv31"))
                        act.activation(u_sb[d], dt_sb[d][:], ACT.Abs).then_inc(done, 1)
                    elif name == "exp":
                        act.wait_ge(done, act_side.done(at, part, "abs"))
                        act.activation(u_sb[d], u_sb[d], ACT.Exp, scale=-1.0).then_inc(done, 1)
                    elif name == "one":
                        act.wait_ge(done, act_side.done(at, part, "exp"))
                        act.activation(sz_sb[d][:], u_sb[d], ACT.Identity, bias=one[:]).then_inc(done, 1)
                    elif name == "ln":
                        act.wait_ge(dve_side.sem, dve_side.done(at, part, "rest"))
                        act.activation(sz_sb[d][:], sz_sb[d][:], ACT.Ln).then_inc(done, 1)
                    elif kind == "Z":
                        after_pe(pe_p)
                        if m == 0:
                            act.wait_ge(dve_side.sem, dve_side.done(at, part, "dt"))
                        act.activation(sz_sb[d][:, m, :], p_ps[:], ACT.Copy).then_inc(done, 1)
                    else:
                        act.wait_ge(done, act_side.done(at, part, "Z3"))
                        act.activation(sz_sb[d][:], sz_sb[d][:], ACT.Silu).then_inc(done, 1)
                elif name[0] == "N":
                    after_pe(pe_q)
                    act.activation(n_t[:, int(name[1]), :], q_ps[:], ACT.Copy).then_inc(done, 1)
                elif name[0] == "F":
                    after_pe(pe_q)
                    j = int(name[1:])
                    act.activation((hid2 if j % 2 else hid1)[:, j // 2, :], q_ps[:], ACT.Identity,
                                   scale=scales[:, j % 2, j // 2:j // 2 + 1]).then_inc(done, 1)
                elif name in ("silu0", "silu1"):
                    i = int(name[4])
                    act.wait_ge(done, act_side.done(at, part, f"F{HC * (i + 1) - 1}"))
                    h = hid1[:, 4 * i:4 * i + 4, :]
                    act.activation(h, h, ACT.Silu).then_inc(done, 1)
                elif name[0] in "HG":
                    after_pe(pe_q)
                    m, s = int(name[1]), 2 if name[0] == "H" else 3
                    if name == "H0":
                        act.wait_ge(dve_side.sem, dve_side.done(at, part, "glu3"))
                    act.activation((hid2 if s == 2 else hid1)[:, m, :], q_ps[:], ACT.Identity,
                                   scale=scales[:, s, m:m + 1]).then_inc(done, 1)
                elif name.startswith("gelu"):
                    i = int(name[4])
                    act.wait_ge(done, act_side.done(at, part, f"{'HG'[i // 2]}{4 * (i % 2) + 3}"))
                    h = (hid2 if i < 2 else hid1)[:, 4 * (i % 2):4 * (i % 2) + 4, :]
                    act.activation(h, h, ACT.Gelu).then_inc(done, 1)
                else:
                    after_pe(pe_q)
                    i = "ab".index(name[2])
                    if i == 0 and at.kind != "first":
                        act.wait_ge(pe_q.sem, pe_q.done(at, "early", "N1"))
                    act.activation(o_sb[:, 2 * i:2 * i + 2, :], q_ps[:].rearrange("p (a n) -> p a n", a=2),
                                   ACT.Copy).then_inc(done, 1)

            def copy_c(at, unit):
                act.wait_ge(c_spread, of_body(at, UNITS, unit + 1))
                act.wait_ge(was_read, of_body(at, HALVES, 2 * unit + 2 - 2 * C_RING) + 2 * C_RING)
                act.activation(c_row[:, unit % C_RING, :], c_ps[:], ACT.Copy).then_inc(c_copied, 1)

            def decays(at, unit):
                d, n = unit // N, unit % N
                if n == 0:
                    if d:
                        act.wait_ge(dve_side.sem, dve_side.done(at, "p1", "dt"))
                    else:
                        act.wait_ge(dve_side.sem, dve_side.before(at))
                for h in range(2):
                    q = 2 * unit + h
                    act.wait_ge(scanned, of_body(at, HALVES, last_user(q, DECAY_RING) + 1) + DECAY_RING)
                    for j in range(2):
                        c = 2 * h + j
                        ins = act.activation(decay[:, q % DECAY_RING, j, 1:T], dt_sb[d][:, c, 1:T], ACT.Exp,
                                             scale=a_neg[:, d, c, n:n + 1])
                    ins.then_inc(decayed, 1)

            def body(at):
                for unit in range(UNITS):
                    if at.kind in SCAN_PARTS:
                        copy_c(at, unit)
                        decays(at, unit)
                    side(at, unit)

            bodies(act, body)

        @block.vector
        def _(dve):
            made = [0]

            def setup(ins):
                made[0] += 1
                ins.then_inc(setup_dve, 1)
                dve.wait_ge(setup_dve, made[0])

            dve.sem_inc(scanned, DECAY_RING)
            dve.sem_inc(driven, 1)
            setup(dve.memset(eps[:], EPS))
            setup(dve.memset(one[:], 1.0))
            setup(dve.memset(decay[:, :, :, 0:1], 0.0))
            for u in u_pad:
                setup(dve.memset(u[:, :, 0:PAD], 0.0))
            dve.wait_ge(loaded, 16 * 6)
            dve.wait_ge(setup_pe, 1)
            seg = mod_sb.rearrange("p (s d) -> p s d", s=6)
            seg_a = mod_a.rearrange("p (s d) -> p s d", s=6)
            for j in range(3):
                setup(dve.tensor_copy(mod_sb[:, j * T:(j + 1) * T], y_ps[j][0:BATCH, :]))
            for s in (1, 4):
                setup(dve.tensor_scalar(seg[:, s, :], seg[:, s, :], 1.0, None, ALU.add))
            g, ga = seg[:, 2:6:3, :], seg_a[:, 2:6:3, :]
            setup(dve.scalar_tensor_tensor(ga, g, -1.0, g, ALU.mult, ALU.max))
            setup(dve.tensor_scalar(ga, ga, 0.25, None, ALU.max))
            setup(dve.tensor_scalar(g, g, 0.0, 2.0, ALU.is_ge, ALU.mult))
            setup(dve.scalar_tensor_tensor(g, g, -1.0, ga, ALU.add, ALU.mult))

            def side(at, unit):
                for s, part, name, n in DVE_SIDE:
                    if s == unit and at.has(part):
                        step(at, part, name, n)

            def step(at, part, name, n_ops):
                k = [0]

                def emit(ins, settle=False):
                    ins.then_inc(dve_side.sem, 1)
                    k[0] += 1
                    if settle:
                        dve.wait_ge(dve_side.sem, dve_side.done(at, part, name, k[0] - 1))

                def over_tiles(row):
                    return row.unsqueeze(1).to_broadcast([P, TT, D])

                if name in ("Y0", "Y1"):
                    d = int(name[1])
                    dve.wait_ge(summed, of_body(at, HALVES, 2 * N if d == 0 else 0) + STATE_RING)
                    for c in range(EC):
                        emit(dve.scalar_tensor_tensor(xc_sb[d][:, c, :], xc_sb[d][:, c, :], d_skip[:, d, c:c + 1],
                                                      y_ps[c][:], ALU.mult, ALU.add), c == EC - 1)
                elif name.startswith("gate"):
                    d = int(name[4])
                    dve.wait_ge(act_side.sem, act_side.before(at))
                    dst = u_sb[d] if d == 0 else u_pad[d][:, :, PAD + T - 1:PAD - 1:-1]
                    emit(dve.tensor_tensor(dst, xc_sb[d][:], sz_sb[d][:], ALU.mult))
                elif name in ("O1a", "O1b"):
                    i = "ab".index(name[2])
                    dve.wait_ge(pe_q.sem, pe_q.done(at, part, name))
                    dst = o_sb[:, 2 * i:2 * i + 2, :]
                    emit(dve.tensor_tensor(dst, dst, q_ps[:].rearrange("p (a n) -> p a n", a=2), ALU.add), i == 1)
                elif name[1:2] == "_":
                    kind = name[0]
                    src, dst, scale, shift = {
                        "o": (o_sb, o_sb, ln2w, ln2b), "n": (x_q, o_sb, mod_q[:, 2, :], mod_q[:, 1, :]),
                        "x": (xa, xa, mod_p[:, 1, :], mod_p[:, 0, :]), "h": (xa, xa, ln1w, ln1b)}[kind]
                    i = 0 if part == "next" else 1
                    if name[2:] == "stats":
                        if kind == "x":
                            dve.wait_ge(x_in.sem, x_in.done(at, "next", "x"))
                        for tt in range(TT):
                            emit(dve.bn_stats(stats[:, i, tt, :], src[:, tt, :]), tt == TT - 1)
                    elif name[2:] == "aggr":
                        dve.sem_inc(passed, 1)
                        for tt in range(TT):
                            emit(dve.bn_aggr(mv[:, i, tt, :], stats[:, i, tt, :]), tt == TT - 1)
                    elif name[2:] == "norm":
                        dve.wait_ge(act_side.sem, act_side.done(at, part, kind + "_rstd"))
                        v, r, t = mv[:, i, :, 1], rstd[:, i, :], newton[:, i, :]
                        emit(dve.scalar_tensor_tensor(t, v, EPS, r, ALU.add, ALU.mult), True)
                        emit(dve.tensor_tensor(t, t, r, ALU.mult), True)
                        emit(dve.tensor_scalar(t, t, -0.5, 1.5, ALU.mult, ALU.add), True)
                        emit(dve.tensor_tensor(r, r, t, ALU.mult), True)
                        for tt in range(TT):
                            emit(dve.tensor_scalar(dst[:, tt, :], src[:, tt, :], mv[:, i, tt, 0:1],
                                                   rstd[:, i, tt:tt + 1], ALU.subtract, ALU.mult), tt == TT - 1)
                    elif name[2:] == "scale":
                        if kind == "x":
                            dve.wait_ge(modp_in.sem, modp_in.done(at, "next", "modp"))
                        emit(dve.tensor_tensor(dst[:], dst[:], over_tiles(scale), ALU.mult), True)
                    else:
                        emit(dve.tensor_tensor(dst[:], dst[:], over_tiles(shift), ALU.add), True)
                elif name == "mix0":
                    dve.wait_ge(q_in.sem, q_in.done(at, "early", "q"))
                    emit(dve.tensor_tensor(o_sb[:], o_sb[:], xn_q[:], ALU.add), True)
                elif name == "mix1":
                    emit(dve.tensor_tensor(o_sb[:], o_sb[:], over_tiles(mod_q[:, 0, :]), ALU.mult), True)
                elif name == "mix2":
                    emit(dve.tensor_tensor(x_q[:], x_q[:], o_sb[:], ALU.add), True)
                elif name.startswith("glu"):
                    i = int(name[3])
                    dve.wait_ge(act_side.sem, act_side.done(at, part, f"silu{i // 2}"))
                    h = slice(2 * i, 2 * i + 2)
                    emit(dve.tensor_tensor(hid1[:, h, :], hid1[:, h, :], hid2[:, h, :], ALU.mult))
                elif name == "gb":
                    emit(dve.tensor_tensor(mod_q[:, 3, :], mod_q[:, 3, :], w3s, ALU.mult), True)
                elif name in ("W0", "W1"):
                    i = int(name[1])
                    dve.wait_ge(pe_q.sem, pe_q.done(at, part, name))
                    tmp = hid2[:, i, :].rearrange("p (a n) -> p a n", a=2)
                    emit(dve.tensor_tensor(tmp, q_ps[:].rearrange("p (a n) -> p a n", a=2),
                                           mod_q[:, 3, :].unsqueeze(1).to_broadcast([P, 2, D]), ALU.mult), True)
                    dst = x_q[:, 2 * i:2 * i + 2, :]
                    emit(dve.tensor_tensor(dst, dst, tmp, ALU.add))
                else:
                    d = 1 if part == "p1" else 0
                    if name.startswith("conv"):
                        m, half = int(name[4]), int(name[5])
                        if half == 0:
                            dve.wait_ge(act_side.sem, act_side.done(at, part, f"X{m}"))
                        dst = xc_sb[d][:, m, :]
                        for i in range(2 * half, 2 * half + 2):
                            src, w = u_pad[d][:, m, i:i + T], taps[:, d, m, i:i + 1]
                            if i == 0:
                                emit(dve.tensor_scalar(dst, src, w, conv_b[:, d, m:m + 1], ALU.mult, ALU.add), True)
                            else:
                                emit(dve.scalar_tensor_tensor(dst, src, w, dst, ALU.mult, ALU.add), i < TAPS - 1)
                    elif name == "BC":
                        dve.wait_ge(act_side.sem, act_side.done(at, part, name))
                        for rows_at, to, parts in ((0, N, b_parts[d]), (N, 0, c_parts[d])):
                            emit(dve.tensor_tensor(parts[to:to + N, :], p_ps[rows_at:rows_at + N, :],
                                                   parts[rows_at:rows_at + N, :].bitcast(F32), ALU.subtract))
                    elif name == "rest":
                        dve.wait_ge(act_side.sem, act_side.done(at, part, "one"))
                        emit(dve.scalar_tensor_tensor(u_sb[d], sz_sb[d][:], 1.0, u_sb[d], ALU.subtract, ALU.subtract),
                             True)
                    elif name == "log1p":
                        dve.wait_ge(act_side.sem, act_side.done(at, part, "ln"))
                        emit(dve.tensor_tensor(sz_sb[d][:], sz_sb[d][:], u_sb[d], ALU.subtract), True)
                    elif name == "dt":
                        emit(dve.scalar_tensor_tensor(dt_sb[d][:], dt_sb[d][:], 0.0, sz_sb[d][:], ALU.max, ALU.add),
                             True)
                    else:
                        emit(dve.tensor_tensor(u_sb[d], dt_sb[d][:], xc_sb[d][:], ALU.mult), True)
                assert k[0] == n_ops, (name, k[0], n_ops)

            def drive(at, q):
                unit, h = q // 2, q % 2
                d = unit // N
                if q == 0:
                    dve.wait_ge(dve_side.sem, dve_side.before(at))
                elif q == 2 * N:
                    dve.wait_ge(dve_side.sem, dve_side.done(at, "p1", "u"))
                if h == 0:
                    dve.wait_ge(b_spread, of_body(at, UNITS, unit + 1))
                dve.wait_ge(summed, of_body(at, HALVES, last_user(q, STATE_RING) + 1) + STATE_RING)
                dve.tensor_tensor(state[:, q % STATE_RING], u_sb[d][:, 2 * h:2 * h + 2, :],
                                  b_ps[:].unsqueeze(1).to_broadcast([P, 2, T]), ALU.mult).then_inc(driven, 1)

            def scan(at, q):
                dve.wait_ge(decayed, of_body(at, HALVES, q + 1))
                dve.wait_ge(driven, of_body(at, HALVES, q + 1) + 1)
                flat = state[:, q % STATE_RING].rearrange("p j t -> p (j t)")
                dve.tensor_tensor_scan(flat, decay[:, q % DECAY_RING].rearrange("p j t -> p (j t)"), flat, 0.0,
                                       ALU.mult, ALU.add).then_inc(scanned, 1)

            def body(at):
                scans = at.kind in SCAN_PARTS
                if scans:
                    drive(at, 0)
                for unit in range(UNITS):
                    if scans:
                        for q in (2 * unit, 2 * unit + 1):
                            if q + 1 < HALVES:
                                drive(at, q + 1)
                            scan(at, q)
                    side(at, unit)

            bodies(dve, body)

        @block.gpsimd
        def _(pool):
            pool.sem_inc(was_read, 2 * C_RING)

            def body(at):
                if at.kind not in SCAN_PARTS:
                    return
                for q in range(HALVES):
                    unit = q // 2
                    pool.wait_ge(scanned, of_body(at, HALVES, q + 1) + DECAY_RING)
                    if q % 2 == 0:
                        pool.wait_ge(c_copied, of_body(at, UNITS, unit + 1) + 1)
                    pool.tensor_tensor(state[:, q % STATE_RING], state[:, q % STATE_RING],
                                       c_row[:, unit % C_RING, :].unsqueeze(1).to_broadcast([P, 2, T]),
                                       ALU.mult).then_inc(was_read, 1)

            bodies(pool, body)


_ORDER = ["x", "win", "wxp", "wdt", "wout", "f1", "h1", "h2", "w3", "cols", "rows", "c_t", "wmod", "consts"]


def kernel(**inputs):
    import numpy as np
    import concourse.bacc as bacc
    from concourse.bass_utils import run_bass_kernel_spmd

    g = {k: np.asarray(v) for k, v in inputs.items()}
    m = lambda name: [g[f"L0_attn_m{i}_{name}"] for i in (1, 2)]
    w = lambda name: g[f"L0_ffn_{name}"]
    by_chunk = lambda a, c: a.reshape(c, P, *a.shape[1:]).swapaxes(0, 1)
    both = lambda name: np.stack([by_chunk(a, EC) for a in m(name)], 1).reshape(P, -1)
    hidden = lambda a: a.reshape(HC, P, HC, P).transpose(0, 3, 2, 1)
    ffn_in = np.stack([w("w1_w").reshape(HC, P, DC, P), w("w2_w").reshape(HC, P, DC, P)], 1)
    arrays = {
        "x": g["L0_attn_x"],
        "win": np.stack([a.reshape(2, EC, P, DC, P).transpose(0, 4, 1, 3, 2) for a in m("W_in")]),
        "wxp": np.stack([a.reshape(-1, EC, P).transpose(2, 1, 0) for a in m("W_xp")], 1),
        "wdt": np.stack([a.T for a in m("W_dt")], 1),
        "wout": np.stack([a.reshape(D, EC, P).transpose(2, 1, 0).reshape(P, -1) for a in m("W_out")]),
        "f1": ffn_in.reshape(4, 2, 2, P, DC, P).transpose(0, 5, 1, 2, 4, 3).reshape(4, P, -1),
        "h1": hidden(w("h1_w")).reshape(HC, P, -1),
        "h2": hidden(w("h2_w")).reshape(HC, P, -1),
        "w3": w("w3_w").reshape(D, 2, 4, P).transpose(1, 3, 2, 0).reshape(2, P, -1),
        "cols": np.concatenate([both("A_log"), both("conv_w"), both("conv_b"), both("dt_b"), both("D")]
                               + [by_chunk(w(s), HC) for s in ("w1_s", "w2_s", "h1_s", "h2_s")], 1),
        "rows": np.stack([g["L0_attn_ln1_w"], g["L0_attn_ln1_b"], g["L0_attn_ln2_w"], g["L0_attn_ln2_b"],
                          w("w3_s")]),
        "c_t": by_chunk(g["L0_c"].T, DC),
        "wmod": by_chunk(g["L0_wmod"], DC),
        "consts": np.concatenate([np.eye(P), np.eye(P)[::-1], np.concatenate([np.eye(N)] * 2)], 1).astype(np.float32),
    }
    nc = bacc.Bacc("TRN2", target_bir_lowering=False, num_devices=1)
    data, args = {}, []
    for name in _ORDER:
        a = np.ascontiguousarray(arrays[name])
        data[f"in_{name}"] = a
        args.append(nc.dram_tensor(f"in_{name}", a.shape, mybir.dt.from_np(a.dtype), kind="ExternalInput").ap())
    out = nc.dram_tensor("out", (BATCH, T, D), F32, kind="ExternalOutput").ap()
    adaln_kernel(nc, *args, out)
    r = run_bass_kernel_spmd(nc, [data], core_ids=[0])
    return r.results[0]["out"]
```

```python
from contextlib import ExitStack

import concourse.bass as bass
from concourse import mybir

F32 = mybir.dt.float32
F32R = mybir.dt.float32r
ALU = mybir.AluOpType
ACT = mybir.ActivationFunctionType

P = 128
BATCH, T, D = 16, 512, 256
E = 2 * D
N = 64
RANK = D // 16
HID = 1024
TAPS = 4
EPS = 1e-5
EC = E // P
DC = D // P
HC = HID // P
TT = T // P
PAD = TAPS - 1
UNITS = 2 * N
HALVES = 2 * UNITS
DECAY_RING, STATE_RING, ROW_RING = 3, 7, 3

KIND_PARTS = {
    "pre": ("next",),
    "first": ("o0", "p1", "next"),
    "mid": ("early", "o0", "late", "p1", "next"),
    "last": ("early", "o0", "late", "p1"),
    "tail": ("early", "late"),
}
SCAN_PARTS = ("first", "mid", "last")


FOLDS = (
    (18, 1), (20, 1), (22, 1), (24, 0), (28, 0), (32, 0), (36, 1), (40, 0), (44, 1),
    (48, 0), (52, 1), (56, 1), (60, 1), (62, 1), (72, 0), (72, 1), (76, 1), (80, 0),
    (82, 1), (84, 1), (86, 1), (88, 1), (92, 1), (96, 0), (98, 0), (98, 1), (100, 1),
    (104, 0), (108, 1), (110, 0), (110, 1), (112, 0), (114, 1), (116, 0), (116, 1), (120, 1),
)
P1_AT, X_AT, NEXT_AT = 6, 68, 82
O1_AT, MIX_AT, N_AT, H_AT, O0_AT, G_AT, W_AT = 2, 15, 25, 47, 79, 83, 116
GAP_F, GAP_HG = 8, (4, 4)
GAPS = {"p1": (3, 1, 1), "next": (2, 1, 1)}


def projection_steps(part, s):
    gap_x, gap_d, gap_z = GAPS[part]
    pe = [(s, part, "T0", 1), (s + 1, part, "T1", 1)]
    act = [(s, part, "T0", 1), (s + 1, part, "T1", 1)]
    dve = []
    for m in range(EC):
        pe.append((s + 2 + gap_x * m, part, f"X{m}", 1))
        act.append((s + 2 + gap_x * m, part, f"X{m}", 2))
        dve += [(s + 3 + gap_x * m + i, part, f"conv{m}{i}", 1 + i) for i in range(2)]
    s += 6 + gap_x * (EC - 1)
    act.append((s, part, "xc", 1))
    pe += [(s + 1, part, "BC", 0), (s + 2, part, "BC", 1)]
    act.append((s + 2, part, "BC", 2))
    dve.append((s + 3, part, "BC", 2))
    pe += [(s + 4, part, "L", 0), (s + 5, part, "L", 1)]
    act.append((s + 5, part, "L", 1))
    for m in range(EC):
        pe.append((s + 7 + gap_d * m, part, f"D{m}", 1))
        act.append((s + 7 + gap_d * m, part, f"D{m}", 1))
    s += 8 + gap_d * (EC - 1)
    act += [(s, part, "abs", 1), (s + 1, part, "exp", 1), (s + 2, part, "one", 1)]
    dve.append((s + 4, part, "rest", 1))
    act.append((s + 5, part, "ln", 1))
    dve += [(s + 7, part, "log1p", 1), (s + 8, part, "dt", 1), (s + 9, part, "u", 1)]
    for m in range(EC):
        pe.append((s + 11 + gap_z * m, part, f"Z{m}", 1))
        act.append((s + 11 + gap_z * m, part, f"Z{m}", 1))
    act.append((s + 13 + gap_z * (EC - 1), part, "sz", 1))
    return pe, act, dve


def norm_steps(part, name, s):
    dve = [(s, part, name + "_stats", TT), (s + 1, part, name + "_aggr", TT), (s + 3, part, name + "_norm", 4 + TT),
           (s + 5, part, name + "_scale", 1), (s + 6, part, name + "_shift", 1)]
    return [(s + 2, part, name + "_rstd", 2)], dve


def side_steps():
    pe_p, act, dve, pe_q = [], [], [], []
    dve += [(0, "early", "Y1", EC), (1, "early", "gate1", 1)]
    for i, name in enumerate(("O1a", "O1b")):
        pe_q += [(O1_AT + 2 * i, "early", name, 0), (O1_AT + 1 + 2 * i, "early", name, 1)]
        dve.append((O1_AT + 1 + 2 * i, "early", name, 1))
    dve += [(MIX_AT + i, "early", f"mix{i}", 1) for i in range(3)]
    for k in range(DC):
        pe_q.append((N_AT + k, "early", f"N{k}", 1))
        act.append((N_AT + k, "early", f"N{k}", 1))
    f_at = [N_AT + 3 + GAP_F * j // 8 for j in range(2 * HC)]
    for j in range(2 * HC):
        pe_q.append((f_at[j], "early", f"F{j}", 1))
        act.append((f_at[j], "early", f"F{j}", 1))
    for i in range(2):
        act.append((f_at[8 * i + 7] + 1, "early", f"silu{i}", 1))
        dve += [(f_at[8 * i + 7] + 2 + j, "early", f"glu{2 * i + j}", 1) for j in range(2)]
    for kind, part, s, gap in (("H", "early", H_AT, GAP_HG[0]), ("G", "late", G_AT, GAP_HG[1])):
        for m in range(HC):
            at = s + gap * m
            pe_q += [(at + i * gap // 4, part, f"{kind}{m}", i // 3) for i in range(4)]
            act.append((at + 3 * gap // 4, part, f"{kind}{m}", 1))
            if m % 4 == 3:
                act.append((at + gap, part, f"gelu{m // 4 + 2 * (kind == 'G')}", 1))
    dve += [(64, "o0", "Y0", EC), (65, "o0", "gate0", 1)]
    for i, name in enumerate(("O0a", "O0b")):
        pe_q += [(O0_AT + 2 * i, "o0", name, 0), (O0_AT + 1 + 2 * i, "o0", name, 1)]
        act.append((O0_AT + 1 + 2 * i, "o0", name, 1))
    dve.append((W_AT - 2, "late", "gb", 1))
    for i in range(2):
        pe_q += [(W_AT + 4 * i + j, "late", f"W{i}", j // 3) for j in range(4)]
        dve.append((W_AT + 3 + 4 * i, "late", f"W{i}", 2))
    for part, name, s in (("early", "o", MIX_AT - 7), ("early", "n", MIX_AT + 3), ("next", "x", X_AT), ("next", "h", X_AT + 7)):
        a, c = norm_steps(part, name, s)
        act += a
        dve += c
    for part, s in (("p1", P1_AT), ("next", NEXT_AT)):
        a, b, c = projection_steps(part, s)
        pe_p += a
        act += b
        dve += c
    in_order = lambda steps: sorted(steps, key=lambda x: x[0])
    return in_order(pe_p), in_order(pe_q), in_order(act), in_order(dve)


PE_P, PE_Q, ACT_SIDE, DVE_SIDE = side_steps()
PE_STEPS = sorted([(*x, "p") for x in PE_P] + [(*x, "q") for x in PE_Q], key=lambda x: x[0])

def chunks():
    order = ([("early", "O1", "O1b")] + [("early", f"F{c}", f"F{4 * c + 3}") for c in range(4)]
             + [("early", f"H{m}", f"H{m}") for m in range(HC)] + [("o0", "O0", "O0b")]
             + [("late", f"G{m}", f"G{m}") for m in range(HC)] + [("late", "W0", "W1"), ("late", "W1", "W1")])
    read = {x[1:3]: x[0] for x in PE_Q}
    return [(0 if i < 2 else read[order[i - 2][0], order[i - 2][2]] + 1, *c) for i, c in enumerate(order)]


CHUNKS = chunks()


class At:

    def __init__(self, b, kind):
        self.b, self.kind = b, kind

    def has(self, part):
        return part in KIND_PARTS[self.kind]


class Signal:

    def __init__(self, sem, steps, by=1):
        self.sem, self.by = sem, by
        self.steps = steps
        self.total = {k: sum(n for _, part, _, n in steps if part in parts) for k, parts in KIND_PARTS.items()}

    def before(self, at):
        t = self.total
        ahead = {"pre": 0, "first": t["pre"], "mid": t["pre"] + t["first"],
                 "last": t["pre"] + t["first"] + (BATCH - 2) * t["mid"]}
        ahead["tail"] = ahead["last"] + t["last"]
        if at.kind == "mid":
            return (at.b - 1) * (t["mid"] * self.by) + ahead["mid"] * self.by
        return ahead[at.kind] * self.by

    def done(self, at, part, name, k=None):
        count = 0
        for _, p, n, ops in self.steps:
            if p not in KIND_PARTS[at.kind]:
                continue
            if (p, n) == (part, name) and ops:
                return self.before(at) + self.by * (count + (ops if k is None else k + 1))
            count += ops
        raise KeyError((part, name))


def adaln_kernel(nc, x, win, wxp, wdt, wout, f1, h1, h2, w3, cols, rows, c_t, wmod, consts, out):
    ctx = ExitStack()
    with ctx:
        def sb(name, shape, dt=F32):
            return ctx.enter_context(nc.sbuf_tensor(name, shape, dt))

        def sem(name):
            return ctx.enter_context(nc.semaphore(name))

        mod_dram = nc.dram_tensor("mod_rows", (BATCH, 6, D), F32, kind="Internal").ap()
        xn_dram = nc.dram_tensor("xn_rows", (BATCH, T, D), F32, kind="Internal").ap()

        wxp_sb = sb("wxp_sb", [P, 2, EC, RANK + 2 * N])
        cols_sb = sb("cols_sb", [P, 2 * EC * N + 2 * EC * TAPS + 3 * 2 * EC + 4 * HC])
        o = 2 * EC * N
        a_neg = cols_sb[:, 0:o].rearrange("p (d c n) -> p d c n", d=2, c=EC)
        taps = cols_sb[:, o:o + 2 * EC * TAPS].rearrange("p (d c k) -> p d c k", d=2, c=EC)
        o += 2 * EC * TAPS
        conv_b, dt_b, d_skip = (cols_sb[:, o + 2 * EC * i:o + 2 * EC * (i + 1)].rearrange("p (d c) -> p d c", d=2)
                                for i in range(3))
        o += 3 * 2 * EC
        scales = cols_sb[:, o:o + 4 * HC].rearrange("p (s c) -> p s c", s=4)
        rows_sb = sb("rows_sb", [P, 5, D])
        ln1w, ln1b, ln2w, ln2b, w3s = (rows_sb[:, i, :] for i in range(5))
        consts_sb = sb("consts_sb", [P, 2 * P + N])
        ident, anti = consts_sb[:, 0:P], consts_sb[:, P:2 * P]
        onehot = sb("onehot", [P, N], F32R)
        eps, one = sb("eps", [P, 1]), sb("one", [P, 1])
        mod_p = sb("mod_p", [P, 2, D])
        mod_q = sb("mod_q", [P, 4, D])
        wp_sb = sb("wp_sb", [P, EC, DC, P])
        wq_sb = sb("wq_sb", [P, 2, 1024])

        decay = sb("decay", [P, DECAY_RING, 2, T])
        state = sb("state", [P, STATE_RING, 2, T])
        rows_sp = sb("rows_sp", [P, ROW_RING, 2, T])

        dt_sb = [sb(f"dt{d}", [P, EC, T]) for d in range(2)]
        xc_sb = [sb(f"xc{d}", [P, EC, T]) for d in range(2)]
        sz_sb = [sb(f"sz{d}", [P, EC, T]) for d in range(2)]
        u_pad = [sb(f"u{d}", [P, EC, PAD + T + 1]) for d in range(2)]
        u_sb = [u[:, :, PAD:PAD + T] for u in u_pad]
        b_parts = [sb(f"b_parts{d}", [P, T], F32R) for d in range(2)]
        c_parts = [sb(f"c_parts{d}", [P, T], F32R) for d in range(2)]

        xa = sb("xa", [P, TT, D])
        x_t = sb("x_t", [P, DC, T])
        o_sb = sb("o_sb", [P, TT, D])
        xn_q = sb("xn_q", [P, TT, D])
        x_q = sb("x_q", [P, TT, D])
        n_t = xn_q[:].rearrange("p a d -> p (a d)").rearrange("p (k t) -> p k t", k=DC)
        hid1 = sb("hid1", [P, HC, T])
        hid2 = sb("hid2", [P, HC, T])
        stats = sb("stats", [P, 2, TT, 6])
        mv = sb("mv", [P, 2, TT, 2])
        ln_v = sb("ln_v", [P, 2, TT])
        rstd = sb("rstd", [P, 2, TT])
        newton = ln_v
        wdt_sb = [sz[0:RANK, 1, :] for sz in sz_sb]
        dt_low = [sz[0:RANK, 0, :] for sz in sz_sb]
        wmod_sb = hid1[:, 0:6, :].rearrange("p (k a) t -> p k (a t)", k=DC)
        silu_c = xa[:, 0, 0:DC * BATCH].rearrange("p (k b) -> p k b", k=DC)
        mod_sb = hid2[0:BATCH, 0:3, :].rearrange("p a t -> p (a t)")
        mod_a = hid2[0:BATCH, 3:6, :].rearrange("p a t -> p (a t)")

        y_ps = [ctx.enter_context(nc.psum_tensor(f"y_ps{c}", [P, T], F32)) for c in range(EC)]
        rows_ps = ctx.enter_context(nc.psum_tensor("rows_ps", [P, 2, T], F32))
        p_ps = ctx.enter_context(nc.psum_tensor("p_ps", [P, T], F32))
        q_ps = ctx.enter_context(nc.psum_tensor("q_ps", [P, T], F32))

        loaded = sem("loaded")
        setup_act, setup_dve, setup_pe, mod_stored = (sem(n) for n in ("setup_act", "setup_dve", "setup_pe",
                                                                       "mod_stored"))
        passed = sem("passed")
        rows_spread, rows_copied, decayed, driven, scanned, was_read, summed = (
            sem(n) for n in ("rows_spread", "rows_copied", "decayed", "driven", "scanned", "was_read", "summed"))
        pe_p = Signal(sem("pe_p"), PE_P)
        pe_q = Signal(sem("pe_q"), PE_Q)
        act_side = Signal(sem("act_side"), ACT_SIDE)
        dve_side = Signal(sem("dve_side"), DVE_SIDE)
        x_in = Signal(sem("x_in"), [(0, "next", "x", 1)], 16)
        modp_in = Signal(sem("modp_in"), [(0, "next", "modp", 1)], 16)
        xn_out = Signal(sem("xn_out"), [(0, "next", "xn", 1)], 16)
        q_in = Signal(sem("q_in"), [(0, "early", "q", 3)], 16)
        out_stored = Signal(sem("out_stored"), [(0, "late", "out", 1)], 16)
        wp_in = Signal(sem("wp_in"), [(0, "p1", "w0", 1), (1, "p1", "w1", 1), (2, "next", "w0", 1),
                                      (3, "next", "w1", 1)], 16)
        wdt_in = Signal(sem("wdt_in"), [(0, "p1", "wdt", 1), (1, "next", "wdt", 1)], 16)
        mid_slot = {(part, name): (i + 1) % 2 for i, (_, part, name, _) in enumerate(CHUNKS)}

        def chunk_slot(at, part, name):
            if at.kind == "first":
                return 0
            if at.kind == "tail" and part == "late":
                return 1 - mid_slot[part, name]
            return mid_slot[part, name]

        class ChunkSignal:

            def __init__(self):
                self.sems = [sem("wq_in0"), sem("wq_in1")]

            def counts(self, kind):
                at = At(None, kind)
                n = [0, 0]
                for _, part, name, _ in CHUNKS:
                    if at.has(part):
                        n[chunk_slot(at, part, name)] += 1
                return n

            def loaded(self, at, part, name):
                slot, count = chunk_slot(at, part, name), 0
                for _, p, nm, _ in CHUNKS:
                    if at.has(p) and chunk_slot(at, p, nm) == slot:
                        count += 1
                    if (p, nm) == (part, name):
                        break
                first, mid, last = (self.counts(k)[slot] for k in ("first", "mid", "last"))
                if at.kind == "mid":
                    return (at.b - 1) * (16 * mid) + 16 * (first + count)
                ahead = {"first": 0, "last": first + (BATCH - 2) * mid,
                         "tail": first + (BATCH - 2) * mid + last}[at.kind]
                return 16 * (ahead + count)

        wq_in = ChunkSignal()
        folded = {2 * u + h for u, h in FOLDS}
        reads = [(kind, q) for q in range(HALVES) for kind in (("read", "fold") if q - 2 in folded else ("read",))]
        sums = [q for q in range(HALVES) if q not in folded]

        def of_body(at, per_body, index):
            return at.b * per_body + index

        def read_done(at, kind, q):
            back, q = divmod(q, HALVES)
            return of_body(at, len(reads), back * len(reads) + reads.index((kind, q)) + 1) + 2 * ROW_RING

        def slot_free(at, q):
            last = last_user(q, STATE_RING)
            back, last = divmod(last, HALVES)
            if last in folded:
                return was_read, read_done(at, "fold", last + 2 + back * HALVES)
            return summed, of_body(at, len(sums), back * len(sums) + sums.index(last) + 1) + STATE_RING

        def last_user(q, ring, count=HALVES):
            if q >= ring:
                return q - ring
            return max(r for r in range(count) if r % ring == q) - count

        def chunk_view(at, part, name):
            w = wq_sb[:, chunk_slot(at, part, name), :]
            if name[0] in "OW":
                return w.rearrange("p (k n) -> p k n", k=4)
            if name[0] == "F":
                return w.rearrange("p (m w k n) -> p m w k n", m=2, w=2, k=DC)
            return w.rearrange("p (k n) -> p k n", k=HC)

        def bodies(eng, body):
            body(At(-1, "pre"))
            body(At(0, "first"))
            with eng.Fori(1, BATCH - 1) as b:
                body(At(b, "mid"))
            body(At(BATCH - 1, "last"))
            body(At(BATCH, "tail"))

        def last_unit(at):
            return UNITS if at.kind in SCAN_PARTS else 128

        block = ctx.enter_context(nc.Block())

        @block.sync
        def _(sp):
            sp.sem_inc(out_stored.sem, 16)
            sp.dma_start(cols_sb[:], cols).then_inc(loaded, 16)
            sp.dma_start(rows_sb[:], rows.partition_broadcast(P)).then_inc(loaded, 16)
            sp.dma_start(consts_sb[:], consts).then_inc(loaded, 16)
            sp.dma_start(wxp_sb[:], wxp).then_inc(loaded, 16)
            sp.dma_start(silu_c, c_t).then_inc(loaded, 16)
            sp.dma_start(wmod_sb, wmod).then_inc(loaded, 16)
            sp.wait_ge(setup_dve, 14)
            sp.dma_start(mod_dram.rearrange("b s d -> b (s d)"), mod_sb).then_inc(mod_stored, 16)
            sp.wait_ge(mod_stored, 16)

            def wait(s, value):
                sp.wait_ge(s, value)
                sp.sem_inc(passed, 1)

            def rows_of(t, b):
                return t[bass.ds(b, 1)].rearrange("a (tt p) d -> p (a tt) d", p=P)

            def load_wp(at, part, c):
                d = 1 if part == "p1" else 0
                if c == 0:
                    if at.kind != "pre":
                        wait(pe_p.sem, pe_p.before(at) if part == "p1" else pe_p.done(at, "p1", "Z3"))
                else:
                    wait(pe_p.sem, pe_p.done(at, part, "X3"))
                sp.dma_start(wp_sb[:], win[d, c]).then_inc(wp_in.sem, 16)

            def load_wdt(at, part):
                d = 1 if part == "p1" else 0
                wait(dve_side.sem, dve_side.done(at, part, "conv31"))
                sp.dma_start(wdt_sb[d], wdt[:, d, :]).then_inc(wdt_in.sem, 16)

            def load_chunk(at, i):
                _, part, name, _ = CHUNKS[i]
                here = [c for c in CHUNKS if at.has(c[1])]
                slot = chunk_slot(at, part, name)
                same = [c for c in here if chunk_slot(at, c[1], c[2]) == slot]
                j = [c[1:3] for c in same].index((part, name))
                if j:
                    wait(pe_q.sem, pe_q.done(at, same[j - 1][1], same[j - 1][3]))
                elif at.kind != "first":
                    wait(pe_q.sem, pe_q.before(at))
                kind, n = name[0], int(name[1:])
                src = {"O": lambda: wout[n], "F": lambda: f1[n], "H": lambda: h1[n],
                       "G": lambda: h2[n], "W": lambda: w3[n]}[kind]()
                sp.dma_start(wq_sb[:, slot, :], src).then_inc(wq_in.sems[slot], 16)

            def load_next(at):
                if at.kind != "pre":
                    wait(pe_p.sem, pe_p.done(at, "p1", "T1"))
                    wait(xn_out.sem, xn_out.before(at))
                    wait(dve_side.sem, dve_side.before(at))
                nxt = at.b + 1
                sp.dma_start(xa[:], rows_of(x, nxt)).then_inc(x_in.sem, 16)
                sp.dma_start(mod_p[:], mod_dram[bass.ds(nxt, 1), 0:2, :].rearrange("a s d -> (a s) d")
                             .partition_broadcast(P)).then_inc(modp_in.sem, 16)

            def store_xn(at):
                wait(dve_side.sem, dve_side.done(at, "next", "h_shift"))
                sp.dma_start(rows_of(xn_dram, at.b + 1), xa[:]).then_inc(xn_out.sem, 16)

            def load_previous(at):
                wait(out_stored.sem, out_stored.before(at) + 16)
                wait(xn_out.sem, xn_out.before(at))
                prev = at.b - 1
                sp.dma_start(xn_q[:], rows_of(xn_dram, prev)).then_inc(q_in.sem, 16)
                sp.dma_start(x_q[:], rows_of(x, prev)).then_inc(q_in.sem, 16)
                sp.dma_start(mod_q[:], mod_dram[bass.ds(prev, 1), 2:6, :].rearrange("a s d -> (a s) d")
                             .partition_broadcast(P)).then_inc(q_in.sem, 16)

            def store_out(at):
                wait(dve_side.sem, dve_side.done(at, "late", "W1"))
                sp.dma_start(rows_of(out, at.b - 1), x_q[:]).then_inc(out_stored.sem, 16)

            def body(at):
                if at.has("early"):
                    load_previous(at)
                for unit in range(UNITS):
                    for i, c in enumerate(CHUNKS):
                        if c[0] == unit and at.has(c[1]):
                            load_chunk(at, i)
                    if unit == max(P1_AT - 5, 0) and at.has("p1"):
                        load_wp(at, "p1", 0)
                    if unit == P1_AT + 3 + 3 * GAPS["p1"][0] and at.has("p1"):
                        load_wp(at, "p1", 1)
                    if unit == P1_AT + 5 + 3 * GAPS["p1"][0] and at.has("p1"):
                        load_wdt(at, "p1")
                    if unit == X_AT - 8 and at.has("next"):
                        load_next(at)
                    if unit == NEXT_AT - 5 and at.has("next"):
                        load_wp(at, "next", 0)
                    if unit == NEXT_AT - 1 and at.has("next"):
                        store_xn(at)
                    if unit == NEXT_AT + 3 + 3 * GAPS["next"][0] and at.has("next"):
                        load_wp(at, "next", 1)
                    if unit == NEXT_AT + 5 + 3 * GAPS["next"][0] and at.has("next"):
                        load_wdt(at, "next")
                    if unit == W_AT + 8 and at.has("late"):
                        store_out(at)

            bodies(sp, body)
            wait(out_stored.sem, 16 * BATCH + 16)
            wait(xn_out.sem, 16 * BATCH)

        @block.tensor
        def _(pe):
            pe.sem_inc(summed, STATE_RING)
            pe.wait_ge(loaded, 16 * 6)
            pe.wait_ge(setup_act, 1)
            for j in range(3):
                for k in range(DC):
                    mm = pe.matmul(y_ps[j][0:BATCH, :], silu_c[:, k, :], wmod_sb[:, k, j * T:(j + 1) * T],
                                   start=(k == 0), stop=(k == DC - 1))
            mm.then_inc(setup_pe, 1)
            pe.wait_ge(setup_dve, 14)
            pe.wait_ge(setup_act, 4)

            def bank_free(at, stream, part, name):
                steps = [s for s in (PE_P if stream == "p" else PE_Q) if at.has(s[1]) and s[3]]
                j = [s[1:3] for s in steps].index((part, name))
                if j:
                    p, n = steps[j - 1][1:3]
                    by_dve = n in ("BC", "O1a", "O1b", "W0", "W1")
                    who = dve_side if by_dve else act_side
                    pe.wait_ge(who.sem, who.done(at, p, n))
                elif at.kind not in ("pre", "first"):
                    pe.wait_ge(act_side.sem, act_side.before(at))
                    pe.wait_ge(dve_side.sem, dve_side.before(at))
                elif at.kind == "first":
                    pe.wait_ge(act_side.sem, act_side.before(at))

            def project(at, part, name, quarter):
                d = 1 if part == "p1" else 0
                if quarter == 0:
                    bank_free(at, "p", part, name)
                if name[0] == "T":
                    k = int(name[1])
                    if k == 0:
                        if part == "next":
                            pe.wait_ge(dve_side.sem, dve_side.done(at, "next", "h_shift"))
                        else:
                            pe.wait_ge(dve_side.sem, dve_side.before(at))
                    for tt in range(TT):
                        at_t = TT - 1 - tt if d else tt
                        mm = pe.matmul(p_ps[:, at_t * P:(at_t + 1) * P], xa[:, tt, k * P:(k + 1) * P],
                                       anti if d else ident, start=True, stop=True)
                elif name[0] in "XZ":
                    m = int(name[1])
                    if m == 0:
                        pe.wait_ge(wp_in.sem, wp_in.done(at, part, "w0" if name[0] == "X" else "w1"))
                    if name == "X0":
                        pe.wait_ge(act_side.sem, act_side.done(at, part, "T1"))
                    for k in range(DC):
                        mm = pe.matmul(p_ps[:], wp_sb[:, m, k, :], x_t[:, k, :], start=(k == 0), stop=(k == DC - 1))
                elif name in ("BC", "L"):
                    if name == "BC" and quarter == 0:
                        pe.wait_ge(act_side.sem, act_side.done(at, part, "xc"))
                    for k in range(2 * quarter, 2 * quarter + 2):
                        if name == "L":
                            mm = pe.matmul(p_ps[0:RANK, :], wxp_sb[:, d, k, 0:RANK], xc_sb[d][:, k, :],
                                           start=(k == 0), stop=(k == EC - 1))
                        else:
                            mm = pe.matmul(p_ps[:], wxp_sb[:, d, k, RANK:RANK + P], xc_sb[d][:, k, :],
                                           start=(k == 0), stop=(k == EC - 1))
                elif name[0] == "D":
                    m = int(name[1])
                    if m == 0:
                        pe.wait_ge(act_side.sem, act_side.done(at, part, "L"))
                        pe.wait_ge(wdt_in.sem, wdt_in.done(at, part, "wdt"))
                    mm = pe.matmul(p_ps[:], wdt_sb[d][:, m * P:(m + 1) * P], dt_low[d], start=True, stop=True)
                return mm

            def network(at, part, name, quarter):
                kind, n = name[0], name[1:]
                if quarter == 0:
                    bank_free(at, "q", part, name)
                if kind == "O":
                    d, half = int(n[0]), "ab".index(n[1])
                    if half == 0 and quarter == 0:
                        pe.wait_ge(dve_side.sem, dve_side.done(at, part, f"gate{d}"))
                        pe.wait_ge(wq_in.sems[chunk_slot(at, part, f"O{d}")], wq_in.loaded(at, part, f"O{d}"))
                    w = chunk_view(at, part, f"O{d}")
                    for k in range(EC):
                        tt = 2 * half + quarter
                        mm = pe.matmul(q_ps[:, quarter * D:(quarter + 1) * D], u_sb[d][:, k, tt * P:(tt + 1) * P],
                                       w[:, k, :], start=(k == 0), stop=(k == EC - 1))
                elif kind == "N":
                    k = int(n)
                    if k == 0:
                        pe.wait_ge(dve_side.sem, dve_side.done(at, part, "n_shift"))
                    for tt in range(TT):
                        mm = pe.matmul(q_ps[:, tt * P:(tt + 1) * P], o_sb[:, tt, k * P:(k + 1) * P], ident,
                                       start=True, stop=True)
                elif kind == "F":
                    j = int(n)
                    m, which = j // 2, j % 2
                    if j == 0:
                        pe.wait_ge(act_side.sem, act_side.done(at, part, "N1"))
                    if j % 4 == 0:
                        pe.wait_ge(wq_in.sems[chunk_slot(at, part, f"F{j // 4}")], wq_in.loaded(at, part, f"F{j // 4}"))
                    w = chunk_view(at, part, f"F{j // 4}")
                    for k in range(DC):
                        mm = pe.matmul(q_ps[:], w[:, m % 2, which, k, :], n_t[:, k, :], start=(k == 0), stop=(k == DC - 1))
                elif kind in "HG":
                    m, src = int(n), (hid1 if kind == "H" else hid2)
                    if quarter == 0:
                        if m == 0 and kind == "H":
                            pe.wait_ge(dve_side.sem, dve_side.done(at, part, "glu3"))
                        if m == 0 and kind == "G":
                            pe.wait_ge(act_side.sem, act_side.done(at, "early", "gelu1"))
                        pe.wait_ge(wq_in.sems[chunk_slot(at, part, name)], wq_in.loaded(at, part, name))
                    w = chunk_view(at, part, name)
                    for k in range(2 * quarter, 2 * quarter + 2):
                        mm = pe.matmul(q_ps[:], w[:, k, :], src[:, k, :], start=(k == 0), stop=(k == HC - 1))
                else:
                    i = int(n)
                    if i == 0 and quarter == 0:
                        pe.wait_ge(act_side.sem, act_side.done(at, part, "gelu3"))
                        for name in ("W0", "W1"):
                            pe.wait_ge(wq_in.sems[chunk_slot(at, part, name)], wq_in.loaded(at, part, name))
                    ws = [chunk_view(at, part, "W0"), chunk_view(at, part, "W1")]
                    r, tt = quarter // 2, 2 * i + quarter // 2
                    for k in range(4 * (quarter % 2), 4 * (quarter % 2) + 4):
                        mm = pe.matmul(q_ps[:, r * D:(r + 1) * D], hid1[:, k, tt * P:(tt + 1) * P],
                                       ws[k // 4][:, k % 4, :], start=(k == 0), stop=(k == HC - 1))
                return mm

            def side(at, unit):
                for s, part, name, n, stream in PE_STEPS:
                    if s != unit or not at.has(part):
                        continue
                    first = min(x[0] for x in PE_STEPS if x[1:3] == (part, name))
                    mm = (project if stream == "p" else network)(at, part, name, s - first)
                    if n:
                        mm.then_inc((pe_p if stream == "p" else pe_q).sem, 1)

            def spread(at, unit):
                d, n = unit // N, unit % N
                if n == 0:
                    if d:
                        pe.wait_ge(dve_side.sem, dve_side.done(at, "p1", "BC"))
                    else:
                        pe.wait_ge(dve_side.sem, dve_side.before(at))
                pe.wait_ge(rows_copied, of_body(at, UNITS, unit) + 1)
                w = onehot[:, n:n + 1].to_broadcast([P, P])
                pe.matmul(rows_ps[:, 0, :], w, b_parts[d][:], start=True, stop=True)
                pe.matmul(rows_ps[:, 1, :], w, c_parts[d][:], start=True, stop=True).then_inc(rows_spread, 1)

            def accumulate(at, q):
                at_q = q % HALVES
                if at_q in folded:
                    return
                unit, h = at_q // 2, at_q % 2
                d, n = unit // N, unit % N
                if n == 0 and h == 0:
                    if d:
                        pe.wait_ge(dve_side.sem, dve_side.done(at, "o0", "Y0", EC - 1))
                    elif at.kind != "first":
                        pe.wait_ge(dve_side.sem, dve_side.done(at, "early", "Y1", EC - 1))
                pe.wait_ge(was_read, read_done(at, "fold" if at_q - 2 in folded else "read", q))
                for j in range(2):
                    mm = pe.matmul(y_ps[2 * h + j][:], ident, state[:, at_q % STATE_RING, j, :],
                                   start=(n == 0), stop=(n == N - 1))
                mm.then_inc(summed, 1)

            def body(at):
                scans = at.kind in SCAN_PARTS
                if scans:
                    spread(at, 0)
                    spread(at, 1)
                for unit in range(UNITS):
                    behind = (2 * unit - 2, 2 * unit - 1) if unit or at.kind in ("mid", "last", "tail") else ()
                    if unit == 0:
                        for q in behind:
                            accumulate(at, q)
                    if scans and unit + 2 < UNITS:
                        spread(at, unit + 2)
                    side(at, unit)
                    if scans and unit:
                        for q in behind:
                            accumulate(at, q)

            bodies(pe, body)

        @block.scalar
        def _(act):
            act.sem_inc(rows_copied, 1)
            act.wait_ge(loaded, 16 * 6)
            act.activation(silu_c, silu_c, ACT.Silu).then_inc(setup_act, 1)
            act.activation(onehot[:], consts_sb[:, 2 * P:2 * P + N], ACT.Copy).then_inc(setup_act, 1)
            act.activation(a_neg, a_neg, ACT.Exp).then_inc(setup_act, 1)
            act.wait_ge(setup_act, 3)
            act.activation(a_neg, a_neg, ACT.Copy, scale=-1.0).then_inc(setup_act, 1)
            act.wait_ge(setup_act, 4)
            act.wait_ge(setup_dve, 14)

            def side(at, unit):
                for s, part, name, _ in ACT_SIDE:
                    if s == unit and at.has(part):
                        step(at, part, name)

            def step(at, part, name):
                done = act_side.sem

                def after_pe(signal):
                    act.wait_ge(signal.sem, signal.done(at, part, name))

                if name.endswith("rstd"):
                    i = 0 if part == "next" else 1
                    act.wait_ge(dve_side.sem, dve_side.done(at, part, name[0] + "_aggr"))
                    act.activation(ln_v[:, i, :], mv[:, i, :, 1], ACT.Ln, bias=eps[:]).then_inc(done, 1)
                    act.wait_ge(done, act_side.done(at, part, name, 0))
                    act.activation(rstd[:, i, :], ln_v[:, i, :], ACT.Exp, scale=-0.5).then_inc(done, 1)
                elif part in ("p1", "next"):
                    d = 1 if part == "p1" else 0
                    kind, m = name[0], (int(name[1]) if name[1:].isdigit() else 0)
                    if kind == "T":
                        after_pe(pe_p)
                        act.activation(x_t[:, m, :], p_ps[:], ACT.Copy).then_inc(done, 1)
                    elif kind == "X":
                        after_pe(pe_p)
                        if m == 0 and at.kind != "pre":
                            act.wait_ge(driven, of_body(at, HALVES, 0 if d else 2 * N) + 1)
                            if d == 0:
                                act.wait_ge(pe_q.sem, pe_q.done(at, "o0", "O0b"))
                            elif at.kind != "first":
                                act.wait_ge(pe_q.sem, pe_q.done(at, "early", "O1b"))
                        act.activation(u_sb[d][:, m, :], p_ps[:], ACT.Copy).then_inc(done, 1)
                        act.wait_ge(done, act_side.done(at, part, name, 0))
                        act.activation(xc_sb[d][:, m, :], u_pad[d][:, m, 0:T], ACT.Identity, bias=conv_b[:, d, m:m + 1],
                                       scale=taps[:, d, m, 0:1]).then_inc(done, 1)
                    elif name == "xc":
                        act.wait_ge(dve_side.sem, dve_side.done(at, part, "conv31"))
                        act.activation(xc_sb[d][:], xc_sb[d][:], ACT.Silu).then_inc(done, 1)
                    elif name == "BC":
                        after_pe(pe_p)
                        if at.kind != "pre" and not (d and at.kind == "first"):
                            act.wait_ge(rows_spread, of_body(at, UNITS, 0 if d else N))
                        act.activation(b_parts[d][0:N, :], p_ps[0:N, :], ACT.Copy).then_inc(done, 1)
                        act.activation(c_parts[d][N:P, :], p_ps[N:P, :], ACT.Copy).then_inc(done, 1)
                    elif name == "L":
                        after_pe(pe_p)
                        act.activation(dt_low[d], p_ps[0:RANK, :], ACT.Copy).then_inc(done, 1)
                    elif kind == "D":
                        after_pe(pe_p)
                        if m == 0 and at.kind != "pre" and not (d and at.kind == "first"):
                            act.wait_ge(decayed, of_body(at, HALVES, 0 if d else 2 * N))
                        act.activation(dt_sb[d][:, m, :], p_ps[:], ACT.Identity, bias=dt_b[:, d, m:m + 1]).then_inc(done, 1)
                    elif name == "abs":
                        act.wait_ge(done, act_side.done(at, part, "D3"))
                        act.wait_ge(dve_side.sem, dve_side.done(at, part, "conv31"))
                        act.activation(u_sb[d], dt_sb[d][:], ACT.Abs).then_inc(done, 1)
                    elif name == "exp":
                        act.wait_ge(done, act_side.done(at, part, "abs"))
                        act.activation(u_sb[d], u_sb[d], ACT.Exp, scale=-1.0).then_inc(done, 1)
                    elif name == "one":
                        act.wait_ge(done, act_side.done(at, part, "exp"))
                        act.activation(sz_sb[d][:], u_sb[d], ACT.Identity, bias=one[:]).then_inc(done, 1)
                    elif name == "ln":
                        act.wait_ge(dve_side.sem, dve_side.done(at, part, "rest"))
                        act.activation(sz_sb[d][:], sz_sb[d][:], ACT.Ln).then_inc(done, 1)
                    elif kind == "Z":
                        after_pe(pe_p)
                        if m == 0:
                            act.wait_ge(dve_side.sem, dve_side.done(at, part, "dt"))
                        act.activation(sz_sb[d][:, m, :], p_ps[:], ACT.Copy).then_inc(done, 1)
                    else:
                        act.wait_ge(done, act_side.done(at, part, "Z3"))
                        act.activation(sz_sb[d][:], sz_sb[d][:], ACT.Silu).then_inc(done, 1)
                elif name[0] == "N":
                    after_pe(pe_q)
                    act.activation(n_t[:, int(name[1]), :], q_ps[:], ACT.Copy).then_inc(done, 1)
                elif name[0] == "F":
                    after_pe(pe_q)
                    j = int(name[1:])
                    act.activation((hid2 if j % 2 else hid1)[:, j // 2, :], q_ps[:], ACT.Identity,
                                   scale=scales[:, j % 2, j // 2:j // 2 + 1]).then_inc(done, 1)
                elif name in ("silu0", "silu1"):
                    i = int(name[4])
                    act.wait_ge(done, act_side.done(at, part, f"F{HC * (i + 1) - 1}"))
                    h = hid1[:, 4 * i:4 * i + 4, :]
                    act.activation(h, h, ACT.Silu).then_inc(done, 1)
                elif name[0] in "HG":
                    after_pe(pe_q)
                    m, s = int(name[1]), 2 if name[0] == "H" else 3
                    if name == "H0":
                        act.wait_ge(dve_side.sem, dve_side.done(at, part, "glu3"))
                    act.activation((hid2 if s == 2 else hid1)[:, m, :], q_ps[:], ACT.Identity,
                                   scale=scales[:, s, m:m + 1]).then_inc(done, 1)
                elif name.startswith("gelu"):
                    i = int(name[4])
                    act.wait_ge(done, act_side.done(at, part, f"{'HG'[i // 2]}{4 * (i % 2) + 3}"))
                    h = (hid2 if i < 2 else hid1)[:, 4 * (i % 2):4 * (i % 2) + 4, :]
                    act.activation(h, h, ACT.Gelu).then_inc(done, 1)
                else:
                    after_pe(pe_q)
                    i = "ab".index(name[2])
                    if i == 0 and at.kind != "first":
                        act.wait_ge(pe_q.sem, pe_q.done(at, "early", "N1"))
                    act.activation(o_sb[:, 2 * i:2 * i + 2, :], q_ps[:].rearrange("p (a n) -> p a n", a=2),
                                   ACT.Copy).then_inc(done, 1)

            def copy_rows(at, unit):
                act.wait_ge(rows_spread, of_body(at, UNITS, unit + 1))
                act.wait_ge(was_read, read_done(at, "read", 2 * last_user(unit, ROW_RING, UNITS) + 1))
                act.activation(rows_sp[:, unit % ROW_RING], rows_ps[:], ACT.Copy).then_inc(rows_copied, 1)

            def decays(at, unit):
                d, n = unit // N, unit % N
                if n == 0:
                    if d:
                        act.wait_ge(dve_side.sem, dve_side.done(at, "p1", "dt"))
                    else:
                        act.wait_ge(dve_side.sem, dve_side.before(at))
                for h in range(2):
                    q = 2 * unit + h
                    act.wait_ge(scanned, of_body(at, HALVES, last_user(q, DECAY_RING) + 1) + DECAY_RING)
                    for j in range(2):
                        c = 2 * h + j
                        ins = act.activation(decay[:, q % DECAY_RING, j, 1:T], dt_sb[d][:, c, 1:T], ACT.Exp,
                                             scale=a_neg[:, d, c, n:n + 1])
                    ins.then_inc(decayed, 1)

            def body(at):
                scans = at.kind in SCAN_PARTS
                if scans:
                    copy_rows(at, 0)
                for unit in range(UNITS):
                    if scans:
                        decays(at, unit)
                        if unit + 1 < UNITS:
                            copy_rows(at, unit + 1)
                    if unit:
                        side(at, unit - 1)
                side(at, UNITS - 1)

            bodies(act, body)

        @block.vector
        def _(dve):
            made = [0]

            def setup(ins):
                made[0] += 1
                ins.then_inc(setup_dve, 1)
                dve.wait_ge(setup_dve, made[0])

            dve.sem_inc(scanned, DECAY_RING)
            dve.sem_inc(driven, 1)
            setup(dve.memset(eps[:], EPS))
            setup(dve.memset(one[:], 1.0))
            setup(dve.memset(decay[:, :, :, 0:1], 0.0))
            for u in u_pad:
                setup(dve.memset(u[:, :, 0:PAD], 0.0))
            dve.wait_ge(loaded, 16 * 6)
            dve.wait_ge(setup_pe, 1)
            seg = mod_sb.rearrange("p (s d) -> p s d", s=6)
            seg_a = mod_a.rearrange("p (s d) -> p s d", s=6)
            for j in range(3):
                setup(dve.tensor_copy(mod_sb[:, j * T:(j + 1) * T], y_ps[j][0:BATCH, :]))
            for s in (1, 4):
                setup(dve.tensor_scalar(seg[:, s, :], seg[:, s, :], 1.0, None, ALU.add))
            g, ga = seg[:, 2:6:3, :], seg_a[:, 2:6:3, :]
            setup(dve.scalar_tensor_tensor(ga, g, -1.0, g, ALU.mult, ALU.max))
            setup(dve.tensor_scalar(ga, ga, 0.25, None, ALU.max))
            setup(dve.tensor_scalar(g, g, 0.0, 2.0, ALU.is_ge, ALU.mult))
            setup(dve.scalar_tensor_tensor(g, g, -1.0, ga, ALU.add, ALU.mult))

            def side(at, unit):
                for s, part, name, n in DVE_SIDE:
                    if s == unit and at.has(part):
                        step(at, part, name, n)

            def step(at, part, name, n_ops):
                k = [0]

                def emit(ins, settle=False):
                    ins.then_inc(dve_side.sem, 1)
                    k[0] += 1
                    if settle:
                        dve.wait_ge(dve_side.sem, dve_side.done(at, part, name, k[0] - 1))

                def over_tiles(row):
                    return row.unsqueeze(1).to_broadcast([P, TT, D])

                if name in ("Y0", "Y1"):
                    d = int(name[1])
                    dve.wait_ge(summed, of_body(at, len(sums), sums.index(2 * N) if d == 0 else 0) + STATE_RING)
                    for c in range(EC):
                        emit(dve.scalar_tensor_tensor(xc_sb[d][:, c, :], xc_sb[d][:, c, :], d_skip[:, d, c:c + 1],
                                                      y_ps[c][:], ALU.mult, ALU.add), c == EC - 1)
                elif name.startswith("gate"):
                    d = int(name[4])
                    dve.wait_ge(act_side.sem, act_side.before(at))
                    dst = u_sb[d] if d == 0 else u_pad[d][:, :, PAD + T - 1:PAD - 1:-1]
                    emit(dve.tensor_tensor(dst, xc_sb[d][:], sz_sb[d][:], ALU.mult))
                elif name in ("O1a", "O1b"):
                    i = "ab".index(name[2])
                    dve.wait_ge(pe_q.sem, pe_q.done(at, part, name))
                    dst = o_sb[:, 2 * i:2 * i + 2, :]
                    emit(dve.tensor_tensor(dst, dst, q_ps[:].rearrange("p (a n) -> p a n", a=2), ALU.add), i == 1)
                elif name[1:2] == "_":
                    kind = name[0]
                    src, dst, scale, shift = {
                        "o": (o_sb, o_sb, ln2w, ln2b), "n": (x_q, o_sb, mod_q[:, 2, :], mod_q[:, 1, :]),
                        "x": (xa, xa, mod_p[:, 1, :], mod_p[:, 0, :]), "h": (xa, xa, ln1w, ln1b)}[kind]
                    i = 0 if part == "next" else 1
                    if name[2:] == "stats":
                        if kind == "x":
                            dve.wait_ge(x_in.sem, x_in.done(at, "next", "x"))
                        for tt in range(TT):
                            emit(dve.bn_stats(stats[:, i, tt, :], src[:, tt, :]), tt == TT - 1)
                    elif name[2:] == "aggr":
                        dve.sem_inc(passed, 1)
                        for tt in range(TT):
                            emit(dve.bn_aggr(mv[:, i, tt, :], stats[:, i, tt, :]), tt == TT - 1)
                    elif name[2:] == "norm":
                        dve.wait_ge(act_side.sem, act_side.done(at, part, kind + "_rstd"))
                        v, r, t = mv[:, i, :, 1], rstd[:, i, :], newton[:, i, :]
                        emit(dve.scalar_tensor_tensor(t, v, EPS, r, ALU.add, ALU.mult), True)
                        emit(dve.tensor_tensor(t, t, r, ALU.mult), True)
                        emit(dve.tensor_scalar(t, t, -0.5, 1.5, ALU.mult, ALU.add), True)
                        emit(dve.tensor_tensor(r, r, t, ALU.mult), True)
                        for tt in range(TT):
                            emit(dve.tensor_scalar(dst[:, tt, :], src[:, tt, :], mv[:, i, tt, 0:1],
                                                   rstd[:, i, tt:tt + 1], ALU.subtract, ALU.mult), tt == TT - 1)
                    elif name[2:] == "scale":
                        if kind == "x":
                            dve.wait_ge(modp_in.sem, modp_in.done(at, "next", "modp"))
                        emit(dve.tensor_tensor(dst[:], dst[:], over_tiles(scale), ALU.mult), True)
                    else:
                        emit(dve.tensor_tensor(dst[:], dst[:], over_tiles(shift), ALU.add), True)
                elif name == "mix0":
                    dve.wait_ge(q_in.sem, q_in.done(at, "early", "q"))
                    emit(dve.tensor_tensor(o_sb[:], o_sb[:], xn_q[:], ALU.add), True)
                elif name == "mix1":
                    emit(dve.tensor_tensor(o_sb[:], o_sb[:], over_tiles(mod_q[:, 0, :]), ALU.mult), True)
                elif name == "mix2":
                    emit(dve.tensor_tensor(x_q[:], x_q[:], o_sb[:], ALU.add), True)
                elif name.startswith("glu"):
                    i = int(name[3])
                    dve.wait_ge(act_side.sem, act_side.done(at, part, f"silu{i // 2}"))
                    h = slice(2 * i, 2 * i + 2)
                    emit(dve.tensor_tensor(hid1[:, h, :], hid1[:, h, :], hid2[:, h, :], ALU.mult))
                elif name == "gb":
                    emit(dve.tensor_tensor(mod_q[:, 3, :], mod_q[:, 3, :], w3s, ALU.mult), True)
                elif name in ("W0", "W1"):
                    i = int(name[1])
                    dve.wait_ge(pe_q.sem, pe_q.done(at, part, name))
                    tmp = hid2[:, i, :].rearrange("p (a n) -> p a n", a=2)
                    emit(dve.tensor_tensor(tmp, q_ps[:].rearrange("p (a n) -> p a n", a=2),
                                           mod_q[:, 3, :].unsqueeze(1).to_broadcast([P, 2, D]), ALU.mult), True)
                    dst = x_q[:, 2 * i:2 * i + 2, :]
                    emit(dve.tensor_tensor(dst, dst, tmp, ALU.add))
                else:
                    d = 1 if part == "p1" else 0
                    if name.startswith("conv"):
                        m, last = int(name[4]), int(name[5])
                        if not last:
                            dve.wait_ge(act_side.sem, act_side.done(at, part, f"X{m}"))
                        dst = xc_sb[d][:, m, :]
                        for i in ((2, 3) if last else (1,)):
                            emit(dve.scalar_tensor_tensor(dst, u_pad[d][:, m, i:i + T], taps[:, d, m, i:i + 1], dst,
                                                          ALU.mult, ALU.add), i < TAPS - 1)
                    elif name == "BC":
                        dve.wait_ge(act_side.sem, act_side.done(at, part, name))
                        for rows_at, to, parts in ((0, N, b_parts[d]), (N, 0, c_parts[d])):
                            emit(dve.tensor_tensor(parts[to:to + N, :], p_ps[rows_at:rows_at + N, :],
                                                   parts[rows_at:rows_at + N, :].bitcast(F32), ALU.subtract))
                    elif name == "rest":
                        dve.wait_ge(act_side.sem, act_side.done(at, part, "one"))
                        emit(dve.scalar_tensor_tensor(u_sb[d], sz_sb[d][:], 1.0, u_sb[d], ALU.subtract, ALU.subtract),
                             True)
                    elif name == "log1p":
                        dve.wait_ge(act_side.sem, act_side.done(at, part, "ln"))
                        emit(dve.tensor_tensor(sz_sb[d][:], sz_sb[d][:], u_sb[d], ALU.subtract), True)
                    elif name == "dt":
                        emit(dve.scalar_tensor_tensor(dt_sb[d][:], dt_sb[d][:], 0.0, sz_sb[d][:], ALU.max, ALU.add),
                             True)
                    else:
                        emit(dve.tensor_tensor(u_sb[d], dt_sb[d][:], xc_sb[d][:], ALU.mult), True)
                assert k[0] == n_ops, (name, k[0], n_ops)

            def drive(at, q):
                unit, h = q // 2, q % 2
                d = unit // N
                if q == 0:
                    dve.wait_ge(dve_side.sem, dve_side.before(at))
                elif q == 2 * N:
                    dve.wait_ge(dve_side.sem, dve_side.done(at, "p1", "u"))
                if h == 0:
                    dve.wait_ge(rows_copied, of_body(at, UNITS, unit + 1) + 1)
                dve.wait_ge(*slot_free(at, q))
                dve.tensor_tensor(state[:, q % STATE_RING], u_sb[d][:, 2 * h:2 * h + 2, :],
                                  rows_sp[:, unit % ROW_RING, 0, :].unsqueeze(1).to_broadcast([P, 2, T]), ALU.mult).then_inc(driven, 1)

            def scan(at, q):
                dve.wait_ge(decayed, of_body(at, HALVES, q + 1))
                dve.wait_ge(driven, of_body(at, HALVES, q + 1) + 1)
                flat = state[:, q % STATE_RING].rearrange("p j t -> p (j t)")
                dve.tensor_tensor_scan(flat, decay[:, q % DECAY_RING].rearrange("p j t -> p (j t)"), flat, 0.0,
                                       ALU.mult, ALU.add).then_inc(scanned, 1)

            def body(at):
                scans = at.kind in SCAN_PARTS
                if scans:
                    drive(at, 0)
                for unit in range(UNITS):
                    if scans:
                        for q in (2 * unit, 2 * unit + 1):
                            if q + 1 < HALVES:
                                drive(at, q + 1)
                            scan(at, q)
                    side(at, unit)

            bodies(dve, body)

        @block.gpsimd
        def _(pool):
            pool.sem_inc(was_read, 2 * ROW_RING)

            def body(at):
                if at.kind not in SCAN_PARTS:
                    return
                for kind, q in reads:
                    unit = q // 2
                    slot, before = state[:, q % STATE_RING], state[:, (q - 2) % STATE_RING]
                    if kind == "fold":
                        pool.wait_ge(was_read, read_done(at, "read", q))
                        pool.tensor_tensor(slot, slot, before, ALU.add).then_inc(was_read, 1)
                        continue
                    pool.wait_ge(scanned, of_body(at, HALVES, q + 1) + DECAY_RING)
                    if q % 2 == 0:
                        pool.wait_ge(rows_copied, of_body(at, UNITS, unit + 1) + 1)
                    pool.tensor_tensor(slot, slot, rows_sp[:, unit % ROW_RING, 1, :].unsqueeze(1).to_broadcast([P, 2, T]),
                                       ALU.mult).then_inc(was_read, 1)

            bodies(pool, body)


_ORDER = ["x", "win", "wxp", "wdt", "wout", "f1", "h1", "h2", "w3", "cols", "rows", "c_t", "wmod", "consts"]


def kernel(**inputs):
    import numpy as np
    import concourse.bacc as bacc
    from concourse.bass_utils import run_bass_kernel_spmd

    g = {k: np.asarray(v) for k, v in inputs.items()}
    m = lambda name: [g[f"L0_attn_m{i}_{name}"] for i in (1, 2)]
    w = lambda name: g[f"L0_ffn_{name}"]
    by_chunk = lambda a, c: a.reshape(c, P, *a.shape[1:]).swapaxes(0, 1)
    both = lambda name: np.stack([by_chunk(a, EC) for a in m(name)], 1).reshape(P, -1)
    hidden = lambda a: a.reshape(HC, P, HC, P).transpose(0, 3, 2, 1)
    ffn_in = np.stack([w("w1_w").reshape(HC, P, DC, P), w("w2_w").reshape(HC, P, DC, P)], 1)
    arrays = {
        "x": g["L0_attn_x"],
        "win": np.stack([a.reshape(2, EC, P, DC, P).transpose(0, 4, 1, 3, 2) for a in m("W_in")]),
        "wxp": np.stack([a.reshape(-1, EC, P).transpose(2, 1, 0) for a in m("W_xp")], 1),
        "wdt": np.stack([a.T for a in m("W_dt")], 1),
        "wout": np.stack([a.reshape(D, EC, P).transpose(2, 1, 0).reshape(P, -1) for a in m("W_out")]),
        "f1": ffn_in.reshape(4, 2, 2, P, DC, P).transpose(0, 5, 1, 2, 4, 3).reshape(4, P, -1),
        "h1": hidden(w("h1_w")).reshape(HC, P, -1),
        "h2": hidden(w("h2_w")).reshape(HC, P, -1),
        "w3": w("w3_w").reshape(D, 2, 4, P).transpose(1, 3, 2, 0).reshape(2, P, -1),
        "cols": np.concatenate([both("A_log"), both("conv_w"), both("conv_b"), both("dt_b"), both("D")]
                               + [by_chunk(w(s), HC) for s in ("w1_s", "w2_s", "h1_s", "h2_s")], 1),
        "rows": np.stack([g["L0_attn_ln1_w"], g["L0_attn_ln1_b"], g["L0_attn_ln2_w"], g["L0_attn_ln2_b"],
                          w("w3_s")]),
        "c_t": by_chunk(g["L0_c"].T, DC),
        "wmod": by_chunk(g["L0_wmod"], DC),
        "consts": np.concatenate([np.eye(P), np.eye(P)[::-1], np.concatenate([np.eye(N)] * 2)], 1).astype(np.float32),
    }
    nc = bacc.Bacc("TRN2", target_bir_lowering=False, num_devices=1)
    data, args = {}, []
    for name in _ORDER:
        a = np.ascontiguousarray(arrays[name])
        data[f"in_{name}"] = a
        args.append(nc.dram_tensor(f"in_{name}", a.shape, mybir.dt.from_np(a.dtype), kind="ExternalInput").ap())
    out = nc.dram_tensor("out", (BATCH, T, D), F32, kind="ExternalOutput").ap()
    adaln_kernel(nc, *args, out)
    r = run_bass_kernel_spmd(nc, [data], core_ids=[0])
    return r.results[0]["out"]
```
